# Optimizing a Trainium2 kernel written in Bass

```python
import numpy as np
import jax
import jax.numpy as jnp

def _softmax(x, axis=-1):
    return jax.nn.softmax(x, axis=axis)
def _gelu(x):
    return jax.nn.gelu(x, approximate=True)
def _silu(x):
    return jax.nn.silu(x)
def _sigmoid(x):
    return jax.nn.sigmoid(x)
def _layernorm(x, axis=-1, eps=1e-5):
    m = jnp.mean(x, axis=axis, keepdims=True)
    v = jnp.var(x, axis=axis, keepdims=True)
    return (x - m) / jnp.sqrt(v + eps)
def _scatter_add(tgt, idx, src, axis=0):
    return tgt.at[idx].add(src)
def _segment_sum(src, seg, n):
    return jax.ops.segment_sum(src, seg, n)

kernel_name = 'mk_adj_preln_d1_adj_128_6d1711'

def setup_inputs(seed: int = 0):
    np.random.seed(seed)
    _w = jnp.asarray
    def _rec_inputs():
        import jax
        import jax.numpy as jnp
        _gk = jax.random.key(seed)
        x = -9.806e-05 + 1 * jax.random.normal(jax.random.fold_in(_gk, 1), (8192, 128), jnp.float32)
        _w = (1.0 + jnp.arange(8192, dtype=jnp.float32)) ** -0.5
        _w = _w / _w.mean()
        _pij = jnp.clip(0.000488281 * _w[:, None] * _w[None, :], 0.0, 1.0)
        _a = jax.random.uniform(jax.random.fold_in(_gk, 2), (8192, 8192)) < _pij
        _a = jnp.logical_or(_a, jnp.eye(8192, dtype=bool))
        _af = _a.astype(jnp.float32)
        _af = _af * jax.random.uniform(jax.random.fold_in(_gk, 3), (8192, 8192), jnp.float32, 0.05, 1)
        adj = _af
        return x, adj
    x, adj = _rec_inputs()
    def _L0_gnn_setup():
        import jax, jax.numpy as jnp
        import numpy as np

        def _lap_mul(A, x):
            d = 1.0 / jnp.sqrt(jnp.sum(A, axis=-1))
            return d[:, None] * (A @ (d[:, None] * x))
        key = jax.random.key(seed)
        k1, k2, k3, k4, k5, k6 = jax.random.split(key, 6)
        N, D_IN, D_OUT = (4096, 128, 128)
        x = jax.random.normal(k1, (N, D_IN), dtype=jnp.float32)
        A = jax.random.uniform(k2, (N, N), dtype=jnp.float32)
        s1 = 1.0 / np.sqrt(D_IN)
        W1 = jax.random.uniform(k3, (D_IN, D_OUT), minval=-s1, maxval=s1, dtype=jnp.float32)
        b1 = jax.random.uniform(k4, (D_OUT,), minval=-s1, maxval=s1, dtype=jnp.float32)
        W2 = jax.random.uniform(k5, (D_IN, D_OUT), minval=-s1, maxval=s1, dtype=jnp.float32)
        b2 = jax.random.uniform(k6, (D_OUT,), minval=-s1, maxval=s1, dtype=jnp.float32)
        return {'x': x, 'A': A, 'W1': W1, 'b1': b1, 'W2': W2, 'b2': b2, 'sigma': 1, 'k': 4}
    _L0_gnn_all = _L0_gnn_setup()
    _L0_gnn_in = {k: v for k, v in _L0_gnn_all.items() if k in ('W1', 'b1', 'W2', 'b2', )}
    del _L0_gnn_all

    return {
        "x": x,
        "adj": adj,
        "L0_gnn_W1": _L0_gnn_in["W1"],
        "L0_gnn_b1": _L0_gnn_in["b1"],
        "L0_gnn_W2": _L0_gnn_in["W2"],
        "L0_gnn_b2": _L0_gnn_in["b2"],
    }

def reference(x, adj, L0_gnn_W1, L0_gnn_b1, L0_gnn_W2, L0_gnn_b2):
    import jax
    import jax.numpy as jnp
    def _L0_gnn_ref(x, A, W1, b1, W2, b2, sigma, k):
        import jax, jax.numpy as jnp
        import numpy as np

        def _lap_mul(A, x):
            d = 1.0 / jnp.sqrt(jnp.sum(A, axis=-1))
            return d[:, None] * (A @ (d[:, None] * x))
        z = _lap_mul(A, x) @ W1 + b1
        z = jax.nn.leaky_relu(z, negative_slope=0.1)
        sq = jnp.sum(z * z, axis=-1)
        d2 = sq[:, None] + sq[None, :] - 2.0 * (z @ z.T)
        d2 = jnp.maximum(d2, 0.0)
        S = jnp.sqrt(d2 + 1e-10)
        S = jnp.exp(-S / (2.0 * sigma))
        order = jnp.argsort(-S, axis=-1)
        ranks = jnp.argsort(order, axis=-1)
        S = jnp.where(ranks < k, S, 0.0)
        A2 = S + A
        out = _lap_mul(A2, x) @ W2 + b2
        return out

    h = jnp.maximum(_layernorm(x, axis=-1), 0.0)
    x = x + _L0_gnn_ref(h, adj, L0_gnn_W1, L0_gnn_b1, L0_gnn_W2, L0_gnn_b2, 1, 4)
    return x


_drawn_inputs = setup_inputs


def setup_inputs(seed=0):
    import zlib

    import numpy as np

    out = dict(_drawn_inputs(seed))
    spreads = {}
    factors = {}
    for name, (base, spread) in spreads.items():
        noise = np.random.default_rng([zlib.crc32(name.encode()), seed]).standard_normal(out[name].shape)
        drawn = base * np.exp(spread * noise) if base else spread * noise
        out[name] = jnp.asarray(drawn.astype(out[name].dtype))
    for name, factor in factors.items():
        out[name] = (out[name] * factor).astype(out[name].dtype)
    return out
```

```python
from contextlib import ExitStack

import concourse.bass as bass
import concourse.mybir as mybir
import numpy as np

P = 128
N = 8192
D = 128
TILES = N // P
SLAB = 512
SLABS = N // SLAB
QT = SLAB // P
QUADS = TILES // QT
GROUPS = 4
SPG = SLABS // GROUPS
QPG = QUADS // GROUPS
RING = 4
BLOCK = QT * SLAB
TOPK = 4
PADT = 2
QUARTER = 2048
QUARTERS = N // QUARTER
EPS_LN = 1e-5
EPS_DIST = 1e-10
SLOPE = 0.1


def build(nc, x, at_blocks, w1, b1, w2, b2, out, w_table):
    f32, bf16, u32 = mybir.dt.float32, mybir.dt.bfloat16, mybir.dt.uint32
    ALU = mybir.AluOpType
    ACT = mybir.ActivationFunctionType
    AX = mybir.AxisListType
    ds = bass.ds

    x_tiles = x.rearrange("(t p) d -> p t d", p=P)
    out_tiles = out.rearrange("(t p) d -> p t d", p=P)
    w_tiles = w_table.rearrange("(t p) d -> p t d", p=P)

    def first_mult(g):
        return QUADS - QPG * g

    def mults_before(g):
        return sum(SPG * QPG * i for i in range(g))

    def sweep2_len(g):
        return QUADS - QPG * g

    def sweep2_before(g):
        return sum(SPG * sweep2_len(i) for i in range(g))

    MULTS1 = mults_before(GROUPS)
    READS1 = SLABS * QUADS
    READS2 = READS1 + sweep2_before(GROUPS)
    MULTS2 = MULTS1 + sweep2_before(GROUPS)
    ADDS = QUADS - 1
    ADD_CREDIT = 4
    MULT_CREDIT = RING
    TURN = 1

    ctx = ExitStack()
    with ctx:
        def sb(name, shape, dt=f32):
            return ctx.enter_context(nc.sbuf_tensor(name, shape, dt))

        def sem(name):
            return ctx.enter_context(nc.semaphore(name))

        zT = sb("zT", [P, N + PADT * P])
        big_a = sb("big_a", [P, N])
        hw2 = sb("hw2", [P, TILES, D])
        ring = sb("ring", [P, RING, BLOCK])
        big_b = sb("big_b", [P, N])
        nsq = sb("nsq", [P, SLAB + N], bf16)
        hw1 = big_a[:, :].rearrange("p (t d) -> p t d", d=D)
        xn = zT[:, 0:N].rearrange("p (t d) -> p t d", d=D)
        rows = [big_a, big_b]
        acc = big_b[:, 0:BLOCK]
        half = big_b[:, 2048:3072]
        colsum = big_b[:, 3072:3584]
        hs = big_b[:, 3584:4096].rearrange("p (c d) -> p c d", d=D)
        hT = big_b[:, 4096:4608]
        diag = big_b[:, 4608:5120]
        d_row = big_b[:, 5120:5632]
        u_sum = big_b[:, 5632:6144]
        z_pre = big_b[:, 6144:6656]
        zsq = big_b[:, 6656:7168]
        rest = big_b[:, 7168:7680]
        gat = big_a[:, 0:QT * TOPK * D]
        near = big_a[:, 2048:2560]
        oT = big_a[:, 2560:3072]
        xs = big_a[:, 3072:3584]
        mix = big_a[:, 3584:4096]
        outs = big_a[:, 4096:4608]

        sq_hi = sb("sq_hi", [P, SLAB], bf16)
        sq_mid = sb("sq_mid", [P, SLAB], bf16)
        ident = sb("ident", [P, P])
        ones = sb("ones", [P, P])
        neg_ones = sb("neg_ones", [P, P])
        part_rows = sb("part_rows", [P, P], bf16)
        w12 = sb("w12", [P, 2, D])
        b1c = sb("b1c", [P, 1])
        b2row = sb("b2row", [P, D])
        b2all = sb("b2all", [P, D])
        eps_ln = sb("eps_ln", [P, 1])
        eps_dist = sb("eps_dist", [P, 1])
        mean = sb("mean", [P, TILES])
        var = sb("var", [P, TILES])
        rstd = sb("rstd", [P, TILES])
        rowsum = sb("rowsum", [P, TILES])
        root = sb("root", [P, TILES])
        newton = sb("newton", [P, TILES])
        deg = sb("deg", [P, TILES])
        deg2 = sb("deg2", [P, TILES])
        near_sum = sb("near_sum", [P, TILES])
        nsq_col = sb("nsq_col", [P, QT + TILES])
        z2 = sb("z2", [P, 2, P])
        top_v = [sb(f"top_v{u}", [P, 8]) for u in range(2)]
        top_i = [sb(f"top_i{u}", [P, 8], u32) for u in range(2)]
        v_all = sb("v_all", [P, PADT + TILES, TOPK])
        i_all = sb("i_all", [P, PADT + TILES, TOPK], u32)
        kern = sb("kern", [P, TILES, TOPK])
        gather_i = sb("gather_i", [P, QT * TOPK], u32)

        psum = ctx.enter_context(nc.psum_tensor("psum", [P, 8 * SLAB], f32))

        def bank(i, n=1):
            return psum[:, i * SLAB:(i + n) * SLAB]

        row_ps = bank(7)[:, 0:TILES]

        const_made = sem("const_made")
        row0_clear = sem("row0_clear")
        small_loaded = sem("small_loaded")
        x_loaded = sem("x_loaded")
        block_loaded = [sem(f"block_loaded{i}") for i in range(RING)]
        added = sem("added")
        multiplied = sem("multiplied")
        dve_step = sem("dve_step")
        act_step = sem("act_step")
        centred = sem("centred")
        squared = sem("squared")
        var_made = sem("var_made")
        std_made = sem("std_made")
        normed = sem("normed")
        b2_ps = sem("b2_ps")
        h_made = sem("h_made")
        hT_ps = sem("hT_ps")
        hT_made = sem("hT_made")
        hw_ps = sem("hw_ps")
        hw_saved = sem("hw_saved")
        folded = sem("folded")
        rowsum_ps = sem("rowsum_ps")
        rowsum_saved = sem("rowsum_saved")
        root_made = sem("root_made")
        y_made = sem("y_made")
        partial_saved = sem("partial_saved")
        diag_made = sem("diag_made")
        d_row_ps = sem("d_row_ps")
        d_row_made = sem("d_row_made")
        zsq_made = sem("zsq_made")
        sq_ps = sem("sq_ps")
        sq_hi_made = sem("sq_hi_made")
        sq_rest = sem("sq_rest")
        sq_mid_made = sem("sq_mid_made")
        sq_lo_made = sem("sq_lo_made")
        z_step = sem("z_step")
        z_made = sem("z_made")
        z2_made = sem("z2_made")
        score_ps = sem("score_ps")
        score_saved = sem("score_saved")
        clamped = sem("clamped")
        max_found = sem("max_found")
        row_free = sem("row_free")
        top_saved = sem("top_saved")
        kern_made = sem("kern_made")
        sum2_made = sem("sum2_made")
        root2_made = sem("root2_made")
        w_made = sem("w_made")
        w_stored = sem("w_stored")
        gather_i_made = sem("gather_i_made")
        gathered = sem("gathered")
        near_step = sem("near_step")
        near_made = sem("near_made")
        oT_made = sem("oT_made")
        oT_ps = sem("oT_ps")
        xs_loaded = sem("xs_loaded")
        mix_step = sem("mix_step")
        outs_made = sem("outs_made")
        out_stored = sem("out_stored")

        waits_passed = sem("waits_passed")

        CONSTANTS = 16
        GATHERS = QT * TOPK
        ADD_BASE = ADD_CREDIT

        def wait_alone(eng, signal, value):
            eng.wait_ge(signal, value)
            eng.sem_inc(waits_passed, 1)

        block = ctx.enter_context(nc.Block())

        @block.sync
        def _(sp):
            sp.dma_start(xn, x_tiles).then_inc(x_loaded, 16)
            sp.dma_start(w12[:, 0, :], w1).then_inc(small_loaded, 16)
            sp.dma_start(w12[:, 1, :], w2).then_inc(small_loaded, 16)
            sp.dma_start(b1c[:, :], b1.rearrange("(p a) -> p a", a=1)).then_inc(small_loaded, 16)
            sp.wait_ge(row0_clear, 1)
            sp.dma_start(b2row[0:1, :], b2.rearrange("(a d) -> a d", a=1)).then_inc(small_loaded, 16)

            def load(slab, q, slot):
                sp.dma_start(ring[:, slot, :], at_blocks[slab, q, :, :]).then_inc(block_loaded[slot], 16)

            for g in range(GROUPS):
                with sp.Fori(SPG * g, SPG * (g + 1)) as slab:
                    for pos in range(QUADS):
                        if pos < RING:
                            wait_alone(sp, added, slab * ADDS + (ADD_BASE + pos - 3))
                        else:
                            wait_alone(sp, added, slab * ADDS + (ADD_BASE + max(pos - RING, 1)))
                        if g and pos < RING:
                            wait_alone(sp, multiplied, (slab - SPG * g) * (QPG * g)
                                       + (MULT_CREDIT + mults_before(g) - (3 - pos)))
                        elif g and pos - RING >= first_mult(g):
                            wait_alone(sp, multiplied, (slab - SPG * g) * (QPG * g)
                                       + (MULT_CREDIT + mults_before(g) + pos - RING - first_mult(g) + 1))
                        load(slab, (QPG * g + pos) % QUADS, pos % RING)
            sp.wait_ge(added, ADD_BASE + SLABS * ADDS)
            for g in range(GROUPS):
                n = sweep2_len(g)
                with sp.Fori(SPG * g, SPG * (g + 1)) as slab:
                    for pos in range(n):
                        wait_alone(sp, multiplied, (slab - SPG * g) * n
                                   + (MULTS1 + sweep2_before(g) + pos + 1))
                        load(slab, QPG * g + pos, pos % RING)
            for pos in range(RING):
                sp.wait_ge(multiplied, MULTS2 + pos + 1)
                load(0, pos, pos)
            for part in range(GROUPS):
                sp.wait_ge(w_made, part + 1)
                t = slice(part * TILES // GROUPS, (part + 1) * TILES // GROUPS)
                sp.dma_start(w_tiles[:, t, :], hw2[:, t, :]).then_inc(w_stored, 16)

            def last_pass(slab, first):
                for pos in range(RING if first else 0, QUADS):
                    wait_alone(sp, multiplied, slab * QUADS + (MULTS2 + pos + 1))
                    load(slab, pos, pos % RING)
                    if pos == QUADS // 2:
                        if not first:
                            wait_alone(sp, outs_made, slab)
                        sp.dma_start(xs.rearrange("p (c d) -> p c d", d=D),
                                     x_tiles[:, ds(slab * QT, QT), :]).then_inc(xs_loaded, 16)

            last_pass(0, True)
            with sp.Fori(1, SLABS) as slab:
                last_pass(slab, False)
            sp.wait_ge(w_stored, 16 * GROUPS)
            sp.wait_ge(out_stored, 16 * SLABS)

        @block.gpsimd
        def _(pool):
            nc.gpsimd.memset(b2row[:, :], 0.0).then_inc(row0_clear, 1)
            made = [0]

            def constant(ins):
                made[0] += 1
                ins.then_inc(const_made, 1)
                pool.wait_ge(const_made, made[0])

            constant(nc.gpsimd.memset(ident[:, :], 0.0))
            constant(nc.gpsimd.affine_select(out=ident[:, :], in_=ident[:, :], compare_op=ALU.not_equal, fill=1.0,
                                             base=0, pattern=[[-1, P]], channel_multiplier=1))
            constant(nc.gpsimd.memset(ones[:, :], 1.0))
            constant(nc.gpsimd.memset(neg_ones[:, :], -1.0))
            constant(nc.gpsimd.memset(eps_ln[:, :], EPS_LN))
            constant(nc.gpsimd.memset(eps_dist[:, :], EPS_DIST))
            constant(nc.gpsimd.memset(part_rows[:, :], 0.0))
            for r in (0, 32, 64):
                constant(nc.gpsimd.memset(part_rows[r:r + 1, :], 1.0))
            for u in range(2):
                constant(nc.gpsimd.memset(top_v[u][:, :], 0.0))
                constant(nc.gpsimd.memset(top_i[u][:, :], 0))
            constant(nc.gpsimd.memset(zT[:, N:N + PADT * P], 0.0))
            constant(nc.gpsimd.memset(nsq[96:128, :], 0.0))
            assert made[0] == CONSTANTS

            pool.wait_ge(z_made, SLABS + TURN)
            for u in range(2):
                nc.gpsimd.tensor_tensor(z2[:, u, :], zT[:, u * P:(u + 1) * P], zT[:, u * P:(u + 1) * P],
                                        ALU.add).then_inc(z2_made, 1)
            with pool.Fori(0, TILES // 2) as pair:
                for u in range(2):
                    pool.wait_ge(row_free, pair * 2 + (u + 1))
                    nc.gpsimd.tensor_copy(v_all[:, ds(pair * 2 + u, 1), :].rearrange("p a k -> p (a k)"),
                                          top_v[u][:, 0:TOPK])
                    nc.gpsimd.tensor_copy(i_all[:, ds(pair * 2 + u, 1), :].rearrange("p a k -> p (a k)"),
                                          top_i[u][:, 0:TOPK])
                    for q in range(QUARTERS):
                        wait_alone(pool, score_saved, pair * (2 * QUARTERS) + (u * QUARTERS + q + 1 + 2))
                        part = rows[u][:, q * QUARTER:(q + 1) * QUARTER]
                        nc.gpsimd.tensor_scalar(part, part, 0.0, None, ALU.min).then_inc(clamped, 1)
                    pool.wait_ge(score_ps, pair * (2 * QUARTERS) + (u + 1) * QUARTERS)
                    zt = zT[:, ds(pair * (2 * P) + (u + 2) * P, P)]
                    nc.gpsimd.tensor_tensor(z2[:, u, :], zt, zt, ALU.add).then_inc(z2_made, 1)
            pool.wait_ge(row_free, TILES + 2)
            for u in range(2):
                nc.gpsimd.tensor_copy(v_all[:, TILES + u, :], top_v[u][:, 0:TOPK]).then_inc(top_saved, 1)
                nc.gpsimd.tensor_copy(i_all[:, TILES + u, :], top_i[u][:, 0:TOPK]).then_inc(top_saved, 1)
            pool.wait_ge(top_saved, 4)

            pool.wait_ge(w_stored, 16 * GROUPS)

            def gathers(slab, first):
                if not first:
                    pool.wait_ge(gathered, slab * (16 * GATHERS))
                    pool.wait_ge(near_made, slab)
                nc.gpsimd.tensor_copy(gather_i[:, :],
                                      i_all[:, ds(slab * QT + PADT, QT), :].rearrange("p a k -> p (a k)")
                                      ).then_inc(gather_i_made, 1)
                wait_alone(pool, gather_i_made, slab + 1)
                for c in range(GATHERS):
                    nc.gpsimd.indirect_dma_start(
                        gat[:, c * D:(c + 1) * D], None, w_table[:, :],
                        bass.IndirectOffsetOnAxis(ap=gather_i[:, c:c + 1], axis=0)).then_inc(gathered, 16)

            gathers(0, True)
            with pool.Fori(1, SLABS) as slab:
                gathers(slab, False)

        @block.scalar
        def _(act):
            for signal in (zsq_made, d_row_made):
                act.sem_inc(signal, TURN)
            act.wait_ge(const_made, CONSTANTS)
            act.wait_ge(centred, 1)
            nc.scalar.activation(big_b[:, :], zT[:, 0:N], ACT.Square).then_inc(squared, 1)
            act.wait_ge(var_made, 1)
            nc.scalar.activation(root[:, :], var[:, :], ACT.Sqrt, bias=eps_ln[:, 0:1],
                                 scale=1.0 / D).then_inc(std_made, 1)
            act.wait_ge(b2_ps, 1)
            nc.scalar.activation(b2all[:, :], bank(4)[:, 0:D], ACT.Copy).then_inc(act_step, 1)
            act.wait_ge(normed, 1)
            with act.Fori(0, SLABS) as b:
                nc.scalar.activation(hs, xn[:, ds(b * QT, QT), :], ACT.Relu).then_inc(h_made, 1)
                act.wait_ge(hT_ps, b + 1)
                nc.scalar.activation(hT, bank(4), ACT.Copy).then_inc(hT_made, 1)
                act.wait_ge(hw_ps, b + 1)
                both = bank(5, 2).rearrange("p (c w d) -> p c w d", c=QT, w=2)
                nc.scalar.activation(hw1[:, ds(b * QT, QT), :], both[:, :, 0, :], ACT.Copy).then_inc(hw_saved, 1)
                nc.scalar.activation(hw2[:, ds(b * QT, QT), :], both[:, :, 1, :], ACT.Copy).then_inc(hw_saved, 1)
            for g in range(GROUPS):
                if g:
                    with act.Fori(SPG * g, SPG * (g + 1)) as slab:
                        act.wait_ge(multiplied, (slab - SPG * g + 1) * (QPG * g)
                                    + (MULT_CREDIT + mults_before(g)))
                        nc.scalar.activation(zT[:, ds(slab * SLAB, SLAB)],
                                             psum[:, ds((slab - SPG * g) * SLAB, SLAB)],
                                             ACT.Copy).then_inc(partial_saved, 1)
                tiles = slice(g * SPG * QT, (g + 1) * SPG * QT)
                act.wait_ge(rowsum_saved, g + 1)
                nc.scalar.activation(root[:, tiles], rowsum[:, tiles], ACT.Sqrt).then_inc(root_made, 1)

            def split_squares(turn):
                act.wait_ge(sq_ps, turn + 1)
                nc.scalar.activation(sq_hi[:, :], bank(5), ACT.Copy)
                nc.scalar.activation(nsq[0:32, ds(turn * SLAB, SLAB)], bank(5)[0:32, :], ACT.Copy)
                nc.scalar.activation(nsq_col[:, ds(turn * QT, QT)], bank(6)[:, 0:QT],
                                     ACT.Copy).then_inc(sq_hi_made, 1)
                act.wait_ge(sq_rest, turn + 1 + TURN)
                nc.scalar.activation(sq_mid[:, :], rest, ACT.Copy)
                nc.scalar.activation(nsq[32:64, ds(turn * SLAB, SLAB)], rest[32:64, :],
                                     ACT.Copy).then_inc(sq_mid_made, 1)

            with act.Fori(0, SLABS) as slab:
                split_squares(slab)
                act.wait_ge(d_row_ps, slab + 1 + TURN)
                act.wait_ge(z_made, slab + TURN)
                nc.scalar.activation(d_row, bank(4), ACT.Copy).then_inc(d_row_made, 1)
                act.wait_ge(z_made, slab + 1 + TURN)
                nc.scalar.activation(zsq, zT[:, ds(slab * SLAB, SLAB)], ACT.Square).then_inc(zsq_made, 1)
            split_squares(SLABS)

            act.wait_ge(sq_lo_made, SLABS + 1)
            act.sem_inc(score_saved, 2)
            with act.Fori(0, TILES // 2) as pair:
                for u in range(2):
                    act.wait_ge(row_free, pair * 2 + (u + 1))
                    for q in range(QUARTERS):
                        wait_alone(act, score_ps, pair * (2 * QUARTERS) + (u * QUARTERS + q + 1))
                        nc.scalar.activation(rows[u][:, q * QUARTER:(q + 1) * QUARTER],
                                             bank(4 * (q % 2), 4), ACT.Identity,
                                             bias=nsq_col[:, ds(pair * 2 + (QT + u), 1)]).then_inc(score_saved, 1)
            act.wait_ge(top_saved, 4)
            kv = kern[:, :, :].rearrange("p t k -> p (t k)")
            nc.scalar.activation(kv, v_all[:, PADT:, :].rearrange("p t k -> p (t k)"), ACT.Sqrt,
                                 bias=eps_dist[:, 0:1], scale=-1.0).then_inc(act_step, 1)
            act.wait_ge(act_step, 2)
            nc.scalar.activation(kv, kv, ACT.Exp, scale=-0.5).then_inc(kern_made, 1)
            act.wait_ge(sum2_made, 1)
            nc.scalar.activation(root[:, :], rowsum[:, :], ACT.Sqrt).then_inc(root2_made, 1)

            def store(slab):
                act.wait_ge(outs_made, slab + 1)
                act.dma_start(out_tiles[:, ds(slab * QT, QT), :],
                              outs.rearrange("p (c d) -> p c d", d=D)).then_inc(out_stored, 16)

            with act.Fori(0, SLABS) as slab:
                act.wait_ge(multiplied, (slab + 1) * QUADS + (MULT_CREDIT + MULTS2))
                nc.scalar.activation(oT, bank(0), ACT.Copy).then_inc(oT_made, 1)
                store(slab)

        @block.vector
        def _(dve):
            steps = [0]
            for signal in (folded, sq_rest, z_made):
                dve.sem_inc(signal, TURN)

            def step(ins):
                steps[0] += 1
                ins.then_inc(dve_step, 1)
                dve.wait_ge(dve_step, steps[0])

            dve.wait_ge(x_loaded, 16)
            step(nc.vector.tensor_reduce(mean[:, :], xn, AX.X, ALU.add))
            step(nc.vector.tensor_scalar(mean[:, :], mean[:, :], 1.0 / D, None, ALU.mult))
            nc.vector.tensor_tensor(xn, xn, mean[:, :].unsqueeze(2).to_broadcast([P, TILES, D]),
                                    ALU.subtract).then_inc(centred, 1)
            dve.wait_ge(squared, 1)
            nc.vector.tensor_reduce(var[:, :], big_b[:, :].rearrange("p (t d) -> p t d", d=D),
                                    AX.X, ALU.add).then_inc(var_made, 1)
            dve.wait_ge(std_made, 1)
            step(nc.vector.reciprocal(rstd[:, :], root[:, :]))
            nc.vector.tensor_tensor(xn, xn, rstd[:, :].unsqueeze(2).to_broadcast([P, TILES, D]),
                                    ALU.mult).then_inc(normed, 1)
            dve.wait_ge(normed, 1)
            dve.sem_inc(added, ADD_CREDIT)

            def inverse_root(dst, src, rt, nt):
                step(nc.vector.reciprocal(dst, rt))
                step(nc.vector.tensor_tensor(nt, dst, dst, ALU.mult))
                step(nc.vector.tensor_tensor(nt, nt, src, ALU.mult))
                step(nc.vector.tensor_scalar(nt, nt, -0.5, 1.5, ALU.mult, ALU.add))
                step(nc.vector.tensor_tensor(dst, dst, nt, ALU.mult))

            for g in range(GROUPS):
                with dve.Fori(SPG * g, SPG * (g + 1)) as slab:
                    def loaded(pos):
                        dve.wait_ge(block_loaded[pos % RING], slab * (16 * QUADS // RING) + 16 * (pos // RING + 1))

                    loaded(0)
                    loaded(1)
                    dve.wait_ge(folded, slab * 2 + TURN)
                    nc.vector.tensor_tensor(acc, ring[:, 0, :], ring[:, 1, :], ALU.add).then_inc(added, 1)
                    for pos in range(2, QUADS):
                        loaded(pos)
                        dve.wait_ge(added, slab * ADDS + (ADD_BASE + pos - 1))
                        nc.vector.tensor_tensor(acc, acc, ring[:, pos % RING, :], ALU.add).then_inc(added, 1)
                    dve.wait_ge(added, slab * ADDS + (ADD_BASE + ADDS))
                    nc.vector.tensor_tensor(half, acc[:, 0:1024], acc[:, 1024:2048], ALU.add).then_inc(folded, 1)
                    dve.wait_ge(folded, slab * 2 + 1 + TURN)
                    dve.wait_ge(rowsum_ps, slab + TURN)
                    nc.vector.tensor_tensor(colsum, half[:, 0:512], half[:, 512:1024], ALU.add).then_inc(folded, 1)
                tiles = slice(g * SPG * QT, (g + 1) * SPG * QT)
                dve.wait_ge(rowsum_ps, SPG * (g + 1) + TURN)
                nc.vector.tensor_copy(rowsum[:, tiles], row_ps[:, tiles]).then_inc(rowsum_saved, 1)
                dve.wait_ge(rowsum_saved, g + 1)
                dve.wait_ge(root_made, g + 1)
                inverse_root(deg[:, tiles], rowsum[:, tiles], root[:, tiles], newton[:, tiles])
                dve.wait_ge(hw_saved, 2 * SLABS)
                nc.vector.tensor_tensor(hw1[:, tiles, :], hw1[:, tiles, :],
                                        deg[:, tiles].unsqueeze(2).to_broadcast([P, SPG * QT, D]),
                                        ALU.mult).then_inc(y_made, 1)

            def split_squares(turn):
                dve.wait_ge(sq_hi_made, turn + 1)
                nc.vector.tensor_tensor(rest, bank(5), sq_hi[:, :], ALU.subtract).then_inc(sq_rest, 1)
                dve.wait_ge(sq_mid_made, turn + 1)
                dve.wait_ge(sq_rest, turn + 1 + TURN)
                nc.vector.tensor_tensor(nsq[64:96, ds(turn * SLAB, SLAB)], rest[64:96, :], sq_mid[64:96, :],
                                        ALU.subtract).then_inc(sq_lo_made, 1)

            for g in range(GROUPS):
                zs = 3 if g else 2
                z0 = sum(SPG * (3 if i else 2) for i in range(g))
                with dve.Fori(SPG * g, SPG * (g + 1)) as slab:
                    at = (slab - SPG * g) * zs + z0
                    zt = zT[:, ds(slab * SLAB, SLAB)]
                    up = psum[:, ds((slab - SPG * g) * SLAB, SLAB)]
                    dve.wait_ge(d_row_ps, slab + TURN)
                    nc.vector.tensor_tensor(diag.rearrange("p (c i) -> p c i", c=QT),
                                            ident[:, :].unsqueeze(1).to_broadcast([P, QT, P]),
                                            deg[:, ds(slab * QT, QT)].unsqueeze(2).to_broadcast([P, QT, P]),
                                            ALU.mult).then_inc(diag_made, 1)
                    split_squares(slab)
                    dve.wait_ge(d_row_made, slab + 1 + TURN)
                    dve.wait_ge(multiplied, (slab - SPG * g + 1) * sweep2_len(g)
                                + (MULT_CREDIT + MULTS1 + sweep2_before(g)))
                    if g:
                        dve.wait_ge(partial_saved, (GROUPS - 1) * SPG)
                        nc.vector.tensor_tensor(u_sum, up, zt, ALU.add).then_inc(z_step, 1)
                        dve.wait_ge(z_step, at + 1)
                        nc.vector.tensor_tensor(z_pre, u_sum, d_row, ALU.mult).then_inc(z_step, 1)
                    else:
                        nc.vector.tensor_tensor(z_pre, up, d_row, ALU.mult).then_inc(z_step, 1)
                    dve.wait_ge(z_step, at + (zs - 1))
                    nc.vector.tensor_scalar(u_sum, z_pre, b1c[:, 0:1], None, ALU.add).then_inc(z_step, 1)
                    dve.wait_ge(z_step, at + zs)
                    nc.vector.scalar_tensor_tensor(zt, u_sum, SLOPE, u_sum, ALU.mult, ALU.max).then_inc(z_made, 1)
            split_squares(SLABS)

            dve.wait_ge(sq_lo_made, SLABS + 1)
            dve.sem_inc(row_free, 2)
            with dve.Fori(0, TILES // 2) as pair:
                for u in range(2):
                    wait_alone(dve, clamped, pair * (2 * QUARTERS) + (u + 1) * QUARTERS)
                    nc.vector.max(top_v[u][:, :], rows[u][:, :]).then_inc(max_found, 1)
                    wait_alone(dve, max_found, pair * 2 + (u + 1))
                    nc.vector.max_index(top_i[u][:, :], top_v[u][:, :], rows[u][:, :]).then_inc(row_free, 1)

            dve.wait_ge(kern_made, 1)
            step(nc.vector.tensor_reduce(near_sum[:, :], kern[:, :, :], AX.X, ALU.add))
            step(nc.vector.tensor_tensor(rowsum[:, :], rowsum[:, :], near_sum[:, :], ALU.add))
            dve.sem_inc(sum2_made, 1)
            dve.wait_ge(root2_made, 1)
            inverse_root(deg2[:, :], rowsum[:, :], root[:, :], newton[:, :])
            for part in range(GROUPS):
                t = slice(part * TILES // GROUPS, (part + 1) * TILES // GROUPS)
                nc.vector.tensor_tensor(hw2[:, t, :], hw2[:, t, :],
                                        deg2[:, t].unsqueeze(2).to_broadcast([P, TILES // GROUPS, D]),
                                        ALU.mult).then_inc(w_made, 1)

            def output(slab, first):
                rows4 = "p (c d) -> p c d"
                dve.wait_ge(gathered, slab * (16 * GATHERS) + 16 * GATHERS)
                g3 = gat.rearrange("p (n d) -> p n d", d=D)
                weights = kern[:, ds(slab * QT, QT), :].rearrange("p t k -> p (t k)")
                nc.vector.tensor_tensor(g3, g3, weights.unsqueeze(2).to_broadcast([P, GATHERS, D]),
                                        ALU.mult).then_inc(near_step, 1)
                dve.wait_ge(near_step, slab + 1)
                nc.vector.tensor_reduce(near.rearrange(rows4, d=D),
                                        gat.rearrange("p (c k d) -> p c d k", k=TOPK, d=D),
                                        AX.X, ALU.add).then_inc(near_made, 1)
                dve.wait_ge(near_made, slab + 1)
                dve.wait_ge(oT_ps, slab + 1)
                nc.vector.tensor_tensor(mix, bank(4), near, ALU.add).then_inc(mix_step, 1)
                dve.wait_ge(mix_step, slab * 3 + 1)
                m3 = mix.rearrange(rows4, d=D)
                nc.vector.tensor_tensor(m3, m3, deg2[:, ds(slab * QT, QT)].unsqueeze(2).to_broadcast([P, QT, D]),
                                        ALU.mult).then_inc(mix_step, 1)
                dve.wait_ge(mix_step, slab * 3 + 2)
                nc.vector.tensor_tensor(m3, m3, b2all[:, :].unsqueeze(1).to_broadcast([P, QT, D]),
                                        ALU.add).then_inc(mix_step, 1)
                dve.wait_ge(mix_step, slab * 3 + 3)
                dve.wait_ge(xs_loaded, slab * 16 + 16)
                if not first:
                    dve.wait_ge(out_stored, slab * 16)
                nc.vector.tensor_tensor(outs, mix, xs, ALU.add).then_inc(outs_made, 1)

            output(0, True)
            with dve.Fori(1, SLABS) as slab:
                output(slab, False)

        @block.tensor
        def _(pe):
            for signal in (rowsum_ps, d_row_ps):
                pe.sem_inc(signal, TURN)
            pe.wait_ge(const_made, CONSTANTS)
            pe.wait_ge(small_loaded, 64)
            nc.tensor.matmul(bank(4)[:, 0:D], ones[:, :], b2row[:, :], start=True, stop=True).then_inc(b2_ps, 1)
            pe.wait_ge(act_step, 1)
            pe.sem_inc(multiplied, MULT_CREDIT)

            def prepare(b):
                pe.wait_ge(h_made, b + 1)
                for c in range(QT):
                    ins = nc.tensor.transpose(bank(4)[:, c * P:(c + 1) * P], hs[:, c, :], ident[:, :])
                ins.then_inc(hT_ps, 1)
                pe.wait_ge(hT_made, b + 1)
                for c in range(QT):
                    ins = nc.tensor.matmul(bank(5, 2)[:, c * 2 * D:(c + 1) * 2 * D], hT[:, c * P:(c + 1) * P],
                                           w12[:, :, :].rearrange("p w d -> p (w d)"), start=True, stop=True)
                ins.then_inc(hw_ps, 1)

            def product(dst, weights, q, slot, first, last):
                for c in range(QT):
                    ins = nc.tensor.matmul(dst, weights[:, q * QT + c, :], ring[:, slot, c * SLAB:(c + 1) * SLAB],
                                           start=first and c == 0, stop=last and c == QT - 1)
                ins.then_inc(multiplied, 1)
                return ins

            for g in range(GROUPS):
                if g:
                    pe.wait_ge(y_made, g)
                if g > 1:
                    pe.wait_ge(partial_saved, SPG * (g - 1))
                with pe.Fori(SPG * g, SPG * (g + 1)) as slab:
                    if g == 0:
                        for j in range(SPG):
                            prepare(slab * SPG + j)
                    dst = psum[:, ds((slab - SPG * g) * SLAB, SLAB)]
                    for pos in range(first_mult(g), QUADS):
                        pe.wait_ge(block_loaded[pos % RING], slab * (16 * QUADS // RING) + 16 * (pos // RING + 1))
                        product(dst, hw1, pos - first_mult(g), pos % RING, pos == first_mult(g), pos == QUADS - 1)
                    pe.wait_ge(folded, slab * 2 + 2 + TURN)
                    for c in range(QT):
                        ins = nc.tensor.matmul(row_ps[:, ds(slab * QT + c, 1)], colsum[:, c * P:(c + 1) * P],
                                               ones[:, 0:1], start=True, stop=True)
                    ins.then_inc(rowsum_ps, 1)

            def squares(turn):
                pe.wait_ge(zsq_made, turn + TURN)
                pe.wait_ge(sq_rest, turn + TURN)
                nc.tensor.matmul(bank(5), neg_ones[:, :], zsq, start=True, stop=True)
                for c in range(QT):
                    ins = nc.tensor.matmul(bank(6)[:, c:c + 1], zsq[:, c * P:(c + 1) * P], neg_ones[:, 0:1],
                                           start=True, stop=True)
                ins.then_inc(sq_ps, 1)

            pe.wait_ge(y_made, GROUPS)
            pe.wait_ge(partial_saved, SPG * (GROUPS - 1))
            for g in range(GROUPS):
                n = sweep2_len(g)
                r0 = (READS1 + sweep2_before(g)) // RING
                with pe.Fori(SPG * g, SPG * (g + 1)) as slab:
                    dst = psum[:, ds((slab - SPG * g) * SLAB, SLAB)]
                    if g:
                        pe.wait_ge(z_made, slab - (SPG - 1) + TURN)
                    for pos in range(n):
                        pe.wait_ge(block_loaded[pos % RING],
                                   (slab - SPG * g) * (16 * n // RING) + 16 * (r0 + pos // RING + 1))
                        ins = product(dst, hw1, QPG * g + pos, pos % RING, pos == 0, pos == n - 1)
                        if pos == QPG - 1:
                            squares(slab)
                            pe.wait_ge(diag_made, slab + 1)
                            pe.wait_ge(d_row_made, slab + TURN)
                            nc.tensor.matmul(bank(4), ones[:, :], diag, start=True, stop=True).then_inc(d_row_ps, 1)
            squares(SLABS)

            with pe.Fori(0, TILES // 2) as pair:
                for u in range(2):
                    pe.wait_ge(z2_made, pair * 2 + (u + 1))
                    for q in range(QUARTERS):
                        pe.wait_ge(score_saved, pair * (2 * QUARTERS) + (u * QUARTERS + q + 1))
                        for c in range(4):
                            j = q * QUARTER + c * SLAB
                            nc.tensor.matmul(bank(4 * (q % 2) + c), z2[:, u, :], zT[:, j:j + SLAB],
                                             start=True, stop=False)
                        for c in range(4):
                            j = q * QUARTER + c * SLAB
                            ins = nc.tensor.matmul(bank(4 * (q % 2) + c), part_rows[:, :],
                                                   nsq[:, SLAB + j:2 * SLAB + j], start=False, stop=True)
                        ins.then_inc(score_ps, 1)

            def last_pass(slab, first):
                if not first:
                    pe.wait_ge(oT_made, slab)
                for pos in range(QUADS):
                    if first and pos % QPG == 0:
                        pe.wait_ge(w_made, pos // QPG + 1)
                    pe.wait_ge(block_loaded[pos % RING],
                               slab * (16 * QUADS // RING) + 16 * (READS2 // RING + pos // RING + 1))
                    product(bank(0), hw2, pos, pos % RING, pos == 0, pos == QUADS - 1)
                pe.wait_ge(oT_made, slab + 1)
                if not first:
                    pe.wait_ge(outs_made, slab)
                for c in range(QT):
                    ins = nc.tensor.transpose(bank(4)[:, c * P:(c + 1) * P], oT[:, c * P:(c + 1) * P], ident[:, :])
                ins.then_inc(oT_ps, 1)

            pe.wait_ge(score_saved, 2 + TILES * QUARTERS)
            last_pass(0, True)
            with pe.Fori(1, SLABS) as slab:
                last_pass(slab, False)


def kernel(x, adj, L0_gnn_W1, L0_gnn_b1, L0_gnn_W2, L0_gnn_b2):
    import concourse.bacc as bacc
    from concourse.bass_utils import run_bass_kernel_spmd

    at = np.asarray(adj).T.reshape(QUADS, QT, P, SLABS, SLAB)
    at = np.ascontiguousarray(at.transpose(3, 0, 2, 1, 4)).reshape(SLABS, QUADS, P, BLOCK)
    arrays = {
        "x": np.ascontiguousarray(x), "at_blocks": at,
        "w1": np.ascontiguousarray(L0_gnn_W1), "b1": np.ascontiguousarray(L0_gnn_b1),
        "w2": np.ascontiguousarray(L0_gnn_W2), "b2": np.ascontiguousarray(L0_gnn_b2),
    }
    nc = bacc.Bacc("TRN2", target_bir_lowering=False, num_devices=1)
    f32 = mybir.dt.float32
    aps = {k: nc.dram_tensor(k, list(a.shape), f32, kind="ExternalInput").ap() for k, a in arrays.items()}
    out = nc.dram_tensor("out", [N, D], f32, kind="ExternalOutput").ap()
    w_table = nc.dram_tensor("w_table", [N, D], f32, kind="Internal").ap()
    build(nc, **aps, out=out, w_table=w_table)
    r = run_bass_kernel_spmd(nc, [arrays], core_ids=[0])
    return r.results[0]["out"]
```

```python
from contextlib import ExitStack

import concourse.bass as bass
import concourse.mybir as mybir
import numpy as np

P = 128
N = 8192
D = 128
TILES = N // P
SLAB = 512
SLABS = N // SLAB
QT = SLAB // P
QUADS = TILES // QT
GROUPS = 4
SPG = SLABS // GROUPS
QPG = QUADS // GROUPS
RING = 4
BLOCK = QT * SLAB
HALVES = 2
HALF = BLOCK // HALVES
HIGHS = 4
TOPK = 4
PADT = 2
QUARTER = 2048
QUARTERS = N // QUARTER
EPS_LN = 1e-5
EPS_DIST = 1e-10
SLOPE = 0.1


def build(nc, x, at_blocks, w1, b1, w2, b2, out, w_table, hw2_table):
    f32, f32r, bf16, u32 = mybir.dt.float32, mybir.dt.float32r, mybir.dt.bfloat16, mybir.dt.uint32
    ALU = mybir.AluOpType
    ACT = mybir.ActivationFunctionType
    AX = mybir.AxisListType
    ds = bass.ds

    x_tiles = x.rearrange("(t p) d -> p t d", p=P)
    out_tiles = out.rearrange("(t p) d -> p t d", p=P)
    hw2_tiles = hw2_table.rearrange("(t p) d -> p t d", p=P)
    w_tiles = w_table.rearrange("(t p) d -> p t d", p=P)

    def order1(g):
        others = iter(range(QPG * g, QUADS))
        known = iter(range(QPG * g))
        return [(next(known), True) if pos % QPG in {1: (1,), 2: (1, 3), 3: (1, 2, 3)}.get(g, ()) else
                (next(others), False) for pos in range(QUADS)]

    def mults_through(g, pos):
        return sum(mult for _, mult in order1(g)[:pos + 1])

    def mults_before(g):
        return sum(SPG * QPG * i for i in range(g))

    def sweep2_len(g):
        return QUADS - QPG * g

    def sweep2_before(g):
        return sum(SPG * sweep2_len(i) for i in range(g))

    MULTS1 = mults_before(GROUPS)
    READS1 = SLABS * QUADS
    ADDS = QUADS - 1
    GATHERS = QT * TOPK
    CONSTANTS = 12
    ADD_CREDIT = RING
    MULT_CREDIT = RING
    HALF_CREDIT = HALVES * RING
    TURN = 1

    ctx = ExitStack()
    with ctx:
        def sb(name, shape, dt=f32):
            return ctx.enter_context(nc.sbuf_tensor(name, shape, dt))

        def sem(name):
            return ctx.enter_context(nc.semaphore(name))

        place = [-(-nc.sbuf_base // 32) * 32]

        def room(nbytes):
            place[0] += nbytes
            return place[0] - nbytes

        def at(offset, name, shape, dt=f32):
            return nc.alloc_sbuf_tensor_at(name, shape, dt, offset=offset)

        def sb(name, shape, dt=f32):
            size = int(np.prod(shape[1:])) * {f32: 4, f32r: 4, u32: 4, bf16: 2}[dt]
            return at(room(-(-size // 32) * 32), name, shape, dt)

        r1 = room(4 * (N + PADT * P))
        xu = at(r1, "xu", [P, N])
        z_hi = at(r1, "z_hi", [P, N + PADT * P], f32r)
        w_hi = at(r1, "w_hi", [P, TILES, D], f32r)
        r2 = room(4 * (N + PADT * P))
        acc = at(r2, "acc", [P, BLOCK])
        half = at(r2 + 8192, "half", [P, BLOCK // 2])
        colsum = at(r2 + 12288, "colsum", [P, SLAB])
        hs = at(r2 + 14336, "hs", [P, QT, D])
        hT = at(r2 + 16384, "hT", [P, QT * P])
        square = at(r2 + 18432, "square", [P, QPG * QT, D])
        hw2_out = at(r2 + 18432, "hw2_out", [P, QPG * QT, D])
        z_lo = at(r2, "z_lo", [P, N + PADT * P], f32r)
        w_lo = at(r2, "w_lo", [P, TILES, D], f32r)
        r3 = room(4 * N)
        hw1 = at(r3, "hw1", [P, TILES, D])
        y_lo = at(r3, "y_lo", [P, TILES, D], f32r)
        row0 = at(r3, "row0", [P, N])
        w_all = at(r3, "w_all", [P, TILES, D])
        r4 = room(4 * N)
        y_hi = at(r4, "y_hi", [P, TILES, D], f32r)
        row1 = at(r4, "row1", [P, N])
        gat = at(r4, "gat", [P, QT * TOPK * D])
        near = at(r4 + 8192, "near", [P, QT * D])
        oT = at(r4 + 10240, "oT", [P, SLAB])
        xs = at(r4 + 12288, "xs", [P, QT * D])
        mix = at(r4 + 14336, "mix", [P, QT * D])
        outs = at(r4 + 16384, "outs", [P, QT * D])
        rows = [row0, row1]
        r5 = room(4 * RING * BLOCK)
        ring = at(r5, "ring", [P, RING, BLOCK])
        ring_lo = at(r5, "ring_lo", [P, RING, BLOCK], f32r)
        a_hi = sb("a_hi", [P, HIGHS, HALF], f32r)
        nsq = sb("nsq", [P, N], bf16)
        r6 = room(6 * 4 * SLAB)
        diag = at(r6, "diag", [P, SLAB])
        d_row = at(r6 + 2048, "d_row", [P, SLAB])
        u_sum = at(r6 + 4096, "u_sum", [P, SLAB])
        z_slab = at(r6 + 6144, "z_slab", [P, SLAB])
        zsq = at(r6 + 8192, "zsq", [P, SLAB])
        rest = at(r6 + 10240, "rest", [P, SLAB])
        z2_hi = at(r6, "z2_hi", [P, 2, P], f32r)
        z2_lo = at(r6 + 1024, "z2_lo", [P, 2, P], f32r)
        v_all = at(r6 + 2048, "v_all", [P, PADT + TILES, TOPK])
        i_all = at(r6 + 3584, "i_all", [P, PADT + TILES, TOPK], u32)
        kern = at(r6 + 5120, "kern", [P, TILES, TOPK])
        gather_i = at(r6 + 6144, "gather_i", [P, QT * TOPK], u32)
        top_v = [at(r6 + 6272 + 32 * u, f"top_v{u}", [P, 8]) for u in range(2)]
        top_i = [at(r6 + 6336 + 32 * u, f"top_i{u}", [P, 8], u32) for u in range(2)]
        sq_mid = sb("sq_mid", [P, SLAB], bf16)
        ident = sb("ident", [P, P])
        ones = sb("ones", [P, P])
        neg_ones = sb("neg_ones", [P, P])
        part_rows = sb("part_rows", [P, P], bf16)
        w12 = sb("w12", [P, 2, D])
        b1c = sb("b1c", [P, 1])
        b2row = sb("b2row", [P, D])
        b2all = sb("b2all", [P, D])
        eps_ln = sb("eps_ln", [P, 1])
        eps_dist = sb("eps_dist", [P, 1])
        mean = sb("mean", [P, QPG * QT])
        var = sb("var", [P, QPG * QT])
        std = sb("std", [P, QPG * QT])
        rowsum = sb("rowsum", [P, TILES])
        root = sb("root", [P, TILES])
        newton = sb("newton", [P, TILES])
        deg = sb("deg", [P, TILES])
        deg2 = sb("deg2", [P, TILES])
        near_sum = sb("near_sum", [P, TILES])
        nsq_col = sb("nsq_col", [P, TILES])
        sq_col = sb("sq_col", [P, TILES])
        assert place[0] <= nc.sbuf_usable_end
        xn = xu[:, :].rearrange("p (t d) -> p t d", d=D)

        psum = ctx.enter_context(nc.psum_tensor("psum", [P, 8 * SLAB], f32))

        def bank(i, n=1):
            return psum[:, i * SLAB:(i + n) * SLAB]

        row_ps = bank(7)[:, 0:TILES]

        const_made = sem("const_made")
        row0_clear = sem("row0_clear")
        small_loaded = sem("small_loaded")
        x_loaded = sem("x_loaded")
        block_loaded = [sem(f"block_loaded{i}") for i in range(RING)]
        added = sem("added")
        multiplied = sem("multiplied")
        hi_made = sem("hi_made")
        lo_made = sem("lo_made")
        halves = sem("halves")
        dve_step = sem("dve_step")
        ln_step = sem("ln_step")
        centred = sem("centred")
        squared = sem("squared")
        var_made = sem("var_made")
        std_made = sem("std_made")
        normed = sem("normed")
        b2_ps = sem("b2_ps")
        b2_made = sem("b2_made")
        h_made = sem("h_made")
        hT_ps = sem("hT_ps")
        hT_made = sem("hT_made")
        hw_ps = sem("hw_ps")
        hw_saved = sem("hw_saved")
        hw2_stored = sem("hw2_stored")
        hw2_loaded = sem("hw2_loaded")
        folded = sem("folded")
        rowsum_ps = sem("rowsum_ps")
        rowsum_saved = sem("rowsum_saved")
        root_made = sem("root_made")
        y_made = sem("y_made")
        y_hi_made = sem("y_hi_made")
        y_lo_made = sem("y_lo_made")
        partial_saved = sem("partial_saved")
        diag_made = sem("diag_made")
        d_row_ps = sem("d_row_ps")
        d_row_made = sem("d_row_made")
        u_step = sem("u_step")
        z_scaled = sem("z_scaled")
        z_shifted = sem("z_shifted")
        z_slab_made = sem("z_slab_made")
        zsq_made = sem("zsq_made")
        z_hi_made = sem("z_hi_made")
        z_made = sem("z_made")
        sq_ps = sem("sq_ps")
        sq_hi_made = sem("sq_hi_made")
        sq_rest = sem("sq_rest")
        sq_mid_made = sem("sq_mid_made")
        sq_lo_made = sem("sq_lo_made")
        tops_clear = sem("tops_clear")
        z2_made = sem("z2_made")
        score_ps = sem("score_ps")
        score_saved = sem("score_saved")
        clamped = sem("clamped")
        negated = sem("negated")
        max_found = sem("max_found")
        row_free = sem("row_free")
        top_saved = sem("top_saved")
        dist_made = sem("dist_made")
        kern_made = sem("kern_made")
        sum2_made = sem("sum2_made")
        root2_made = sem("root2_made")
        w_made = sem("w_made")
        w_hi_made = sem("w_hi_made")
        w_lo_made = sem("w_lo_made")
        w_stored = sem("w_stored")
        gather_i_made = sem("gather_i_made")
        gathered = sem("gathered")
        near_step = sem("near_step")
        near_made = sem("near_made")
        oT_made = sem("oT_made")
        oT_ps = sem("oT_ps")
        xs_loaded = sem("xs_loaded")
        mix_step = sem("mix_step")
        outs_made = sem("outs_made")
        out_stored = sem("out_stored")
        waits_passed = sem("waits_passed")

        def wait_alone(eng, signal, value):
            eng.wait_ge(signal, value)
            eng.sem_inc(waits_passed, 1)

        def run(g):
            return (0, sweep2_before(GROUPS), QUADS) if g is None else (SPG * g, sweep2_before(g), sweep2_len(g))

        def number(g, slab, pos):
            first, before, n = run(g)
            return (slab - first) * n + (before + pos)

        def arrived(eng, g, slab, pos):
            first, before, n = run(g)
            eng.wait_ge(block_loaded[pos % RING],
                        (slab - first) * (16 * n // RING) + 16 * ((READS1 + before) // RING + pos // RING + 1))

        def arrived1(eng, slab, pos):
            eng.wait_ge(block_loaded[pos % RING], slab * (16 * QUADS // RING) + 16 * (pos // RING + 1))

        def products_done(eng, g, slab):
            eng.wait_ge(halves, number(g, slab, run(g)[2]) * HALVES + HALF_CREDIT)

        block = ctx.enter_context(nc.Block())

        @block.sync
        def _(sp):
            sp.dma_start(xn, x_tiles).then_inc(x_loaded, 16)
            sp.dma_start(w12[:, 0, :], w1).then_inc(small_loaded, 16)
            sp.dma_start(w12[:, 1, :], w2).then_inc(small_loaded, 16)
            sp.dma_start(b1c[:, :], b1.rearrange("(p a) -> p a", a=1)).then_inc(small_loaded, 16)
            sp.wait_ge(row0_clear, 1)
            sp.dma_start(b2row[0:1, :], b2.rearrange("(a d) -> a d", a=1)).then_inc(small_loaded, 16)

            def load(slab, q, slot):
                sp.dma_start(ring[:, slot, :], at_blocks[slab, q, :, :]).then_inc(block_loaded[slot], 16)

            for g in range(GROUPS):
                with sp.Fori(SPG * g, SPG * (g + 1)) as slab:
                    for pos in range(QUADS):
                        if pos < RING:
                            wait_alone(sp, added, slab * ADDS + (ADD_CREDIT + pos - 3))
                        else:
                            wait_alone(sp, added, slab * ADDS + (ADD_CREDIT + max(pos - RING, 1)))
                        if g and pos < RING:
                            later = min(QPG * h - mults_through(h, pos + QUADS - RING) for h in (g - 1, g))
                            wait_alone(sp, multiplied, (slab - SPG * g) * (QPG * g)
                                       + (MULT_CREDIT + mults_before(g) - later))
                        elif g and order1(g)[pos - RING][1]:
                            wait_alone(sp, multiplied, (slab - SPG * g) * (QPG * g)
                                       + (MULT_CREDIT + mults_before(g) + mults_through(g, pos - RING)))
                        load(slab, order1(g)[pos][0], pos % RING)

            def reload(g, slab, pos):
                wait_alone(sp, halves, number(g, slab, pos) * HALVES + (HALF_CREDIT - HALVES * (RING - 1)))
                load(slab, (QPG * g if g else 0) + pos, pos % RING)

            sp.wait_ge(added, ADD_CREDIT + SLABS * ADDS)
            for g in range(GROUPS):
                with sp.Fori(SPG * g, SPG * (g + 1)) as slab:
                    for pos in range(sweep2_len(g)):
                        if g == 0 and pos < RING:
                            sp.wait_ge(multiplied, MULT_CREDIT + MULTS1 - QPG * (GROUPS - 1)
                                       + mults_through(GROUPS - 1, pos + QUADS - RING))
                        reload(g, slab, pos)
            for pos in range(RING):
                sp.wait_ge(halves, number(None, 0, pos) * HALVES + (HALF_CREDIT - HALVES * (RING - 1)))
                load(0, pos, pos)
            sp.wait_ge(hw2_stored, 16 * GROUPS)
            sp.wait_ge(row_free, 2 + TILES - 1)
            sp.dma_start(w_all[:, :, :], hw2_tiles).then_inc(hw2_loaded, 16)

            def store_w(part):
                sp.wait_ge(w_made, part + 1)
                t = slice(part * TILES // GROUPS, (part + 1) * TILES // GROUPS)
                sp.dma_start(w_tiles[:, t, :], w_all[:, t, :]).then_inc(w_stored, 16)

            def load_x(slab):
                sp.dma_start(xs[:, :].rearrange("p (c d) -> p c d", d=D),
                             x_tiles[:, ds(slab * QT, QT), :]).then_inc(xs_loaded, 16)

            def store_out(slab):
                sp.dma_start(out_tiles[:, ds(slab * QT, QT), :],
                             outs[:, :].rearrange("p (c d) -> p c d", d=D)).then_inc(out_stored, 16)

            store_w(0)
            for part in range(1, GROUPS):
                store_w(part)
                for pos in range(QPG * part, QPG * (part + 1)):
                    reload(None, 0, pos)

            for pos in range(QUADS):
                reload(None, 1, pos)
                if pos == QUADS // 4:
                    load_x(0)
            with sp.Fori(2, SLABS) as slab:
                for pos in range(QUADS):
                    reload(None, slab, pos)
                    if pos == QPG:
                        wait_alone(sp, outs_made, slab - 1)
                        store_out(slab - 2)
                    if pos == QPG + 2:
                        wait_alone(sp, out_stored, (slab - 1) * 16)
                        load_x(slab - 1)
            sp.wait_ge(outs_made, SLABS - 1)
            store_out(SLABS - 2)
            sp.wait_ge(out_stored, 16 * (SLABS - 1))
            load_x(SLABS - 1)
            sp.wait_ge(outs_made, SLABS)
            store_out(SLABS - 1)
            sp.wait_ge(w_stored, 16 * GROUPS)
            sp.wait_ge(out_stored, 16 * SLABS)

        @block.gpsimd
        def _(pool):
            nc.gpsimd.memset(b2row[:, :], 0.0).then_inc(row0_clear, 1)
            made = [0]

            def constant(ins):
                made[0] += 1
                ins.then_inc(const_made, 1)
                pool.wait_ge(const_made, made[0])

            constant(nc.gpsimd.memset(ident[:, :], 0.0))
            constant(nc.gpsimd.affine_select(out=ident[:, :], in_=ident[:, :], compare_op=ALU.not_equal, fill=1.0,
                                             base=0, pattern=[[-1, P]], channel_multiplier=1))
            constant(nc.gpsimd.memset(ones[:, :], 1.0))
            constant(nc.gpsimd.memset(neg_ones[:, :], -1.0))
            constant(nc.gpsimd.memset(eps_ln[:, :], EPS_LN))
            constant(nc.gpsimd.memset(eps_dist[:, :], EPS_DIST))
            constant(nc.gpsimd.memset(part_rows[:, :], 0.0))
            for r in (0, 32, 64):
                constant(nc.gpsimd.memset(part_rows[r:r + 1, :], 1.0))
            constant(nc.gpsimd.memset(z_hi[:, N:N + PADT * P].bitcast(f32), 0.0))
            constant(nc.gpsimd.memset(z_lo[:, N:N + PADT * P].bitcast(f32), 0.0))
            assert made[0] == CONSTANTS

            pool.wait_ge(y_made, GROUPS)
            with pool.Fori(0, SLABS) as slab:
                wait_alone(pool, d_row_ps, slab + TURN)
                nc.gpsimd.tensor_tensor(diag[:, :].rearrange("p (c i) -> p c i", c=QT),
                                        ident[:, :].unsqueeze(1).to_broadcast([P, QT, P]),
                                        deg[:, ds(slab * QT, QT)].unsqueeze(2).to_broadcast([P, QT, P]),
                                        ALU.mult).then_inc(diag_made, 1)

            pool.wait_ge(z_made, SLABS)
            pool.wait_ge(sq_lo_made, SLABS)
            for u in range(2):
                nc.gpsimd.memset(top_v[u][:, :], 0.0).then_inc(tops_clear, 1)
                nc.gpsimd.memset(top_i[u][:, :], 0).then_inc(tops_clear, 1)
                for z2, z in ((z2_hi, z_hi), (z2_lo, z_lo)):
                    zt = z[:, u * P:(u + 1) * P].bitcast(f32)
                    nc.gpsimd.tensor_tensor(z2[:, u, :], zt, zt, ALU.add).then_inc(z2_made, 1)
            pool.wait_ge(tops_clear, 4)
            with pool.Fori(0, TILES // 2) as pair:
                for u in range(2):
                    wait_alone(pool, row_free, pair * 2 + (u + 1))
                    nc.gpsimd.tensor_copy(v_all[:, ds(pair * 2 + u, 1), :].rearrange("p a k -> p (a k)"),
                                          top_v[u][:, 0:TOPK])
                    nc.gpsimd.tensor_copy(i_all[:, ds(pair * 2 + u, 1), :].rearrange("p a k -> p (a k)"),
                                          top_i[u][:, 0:TOPK])
                    for q in range(0, QUARTERS, 2):
                        wait_alone(pool, score_saved, pair * (2 * QUARTERS) + (u * QUARTERS + q + 1 + 2))
                        part = rows[u][:, q * QUARTER:(q + 1) * QUARTER]
                        nc.gpsimd.tensor_scalar(part, part, 0.0, None, ALU.min).then_inc(clamped, 1)
                    wait_alone(pool, score_ps, pair * (2 * QUARTERS) + (u + 1) * QUARTERS)
                    for z2, z in ((z2_hi, z_hi), (z2_lo, z_lo)):
                        zt = z[:, ds(pair * (2 * P) + (u + 2) * P, P)].bitcast(f32)
                        nc.gpsimd.tensor_tensor(z2[:, u, :], zt, zt, ALU.add).then_inc(z2_made, 1)
            pool.wait_ge(row_free, TILES + 2)
            for u in range(2):
                nc.gpsimd.tensor_copy(v_all[:, TILES + u, :], top_v[u][:, 0:TOPK]).then_inc(top_saved, 1)
                nc.gpsimd.tensor_copy(i_all[:, TILES + u, :], top_i[u][:, 0:TOPK]).then_inc(top_saved, 1)
            pool.wait_ge(top_saved, 4)

            pool.wait_ge(w_stored, 16 * GROUPS)

            def gathers(slab, first):
                if not first:
                    pool.wait_ge(gathered, slab * (16 * GATHERS))
                    wait_alone(pool, near_made, slab * QT)
                nc.gpsimd.tensor_copy(gather_i[:, :],
                                      i_all[:, ds(slab * QT + PADT, QT), :].rearrange("p a k -> p (a k)")
                                      ).then_inc(gather_i_made, 1)
                wait_alone(pool, gather_i_made, slab + 1)
                for c in range(GATHERS):
                    nc.gpsimd.indirect_dma_start(
                        gat[:, c * D:(c + 1) * D], None, w_table[:, :],
                        bass.IndirectOffsetOnAxis(ap=gather_i[:, c:c + 1], axis=0)).then_inc(gathered, 16)

            gathers(0, True)
            with pool.Fori(1, SLABS) as slab:
                gathers(slab, False)

        @block.scalar
        def _(act):
            act.sem_inc(d_row_made, TURN)
            act.wait_ge(const_made, CONSTANTS)
            act.wait_ge(b2_ps, 1)
            nc.scalar.activation(b2all[:, :], bank(4)[:, 0:D], ACT.Copy).then_inc(b2_made, 1)
            with act.Fori(0, GROUPS) as part:
                wait_alone(act, centred, part + 1)
                nc.scalar.activation(square[:, :, :], xn[:, ds(part * (QPG * QT), QPG * QT), :],
                                     ACT.Square).then_inc(squared, 1)
                act.wait_ge(var_made, part + 1)
                nc.scalar.activation(std[:, :], var[:, :], ACT.Sqrt, bias=eps_ln[:, 0:1],
                                     scale=1.0 / D).then_inc(std_made, 1)
                wait_alone(act, normed, part + 1)
                for j in range(QPG):
                    b = part * QPG + j
                    nc.scalar.activation(hs[:, :, :], xn[:, ds(b * QT, QT), :], ACT.Relu).then_inc(h_made, 1)
                    act.wait_ge(hT_ps, b + 1)
                    nc.scalar.activation(hT[:, :], bank(4), ACT.Copy).then_inc(hT_made, 1)
                    wait_alone(act, hw_ps, b + 1)
                    both = bank(5, 2).rearrange("p (c w d) -> p c w d", c=QT, w=2)
                    nc.scalar.activation(hw1[:, ds(b * QT, QT), :], both[:, :, 0, :], ACT.Copy).then_inc(hw_saved, 1)
                    nc.scalar.activation(hw2_out[:, j * QT:(j + 1) * QT, :], both[:, :, 1, :],
                                         ACT.Copy).then_inc(hw_saved, 1)
                wait_alone(act, hw_saved, (part + 1) * (2 * QPG))
                act.dma_start(hw2_tiles[:, ds(part * (QPG * QT), QPG * QT), :],
                              hw2_out[:, :, :]).then_inc(hw2_stored, 16)
                wait_alone(act, hw2_stored, part * 16 + 16)
            for g in range(GROUPS):
                if g:
                    with act.Fori(SPG * g, SPG * (g + 1)) as slab:
                        wait_alone(act, multiplied, (slab - SPG * g + 1) * (QPG * g)
                                   + (MULT_CREDIT + mults_before(g)))
                        nc.scalar.activation(xu[:, ds(slab * SLAB, SLAB)],
                                             psum[:, ds((slab - SPG * g) * SLAB, SLAB)],
                                             ACT.Copy).then_inc(partial_saved, 1)
                tiles = slice(g * SPG * QT, (g + 1) * SPG * QT)
                act.wait_ge(rowsum_saved, g + 1)
                nc.scalar.activation(root[:, tiles], rowsum[:, tiles], ACT.Sqrt).then_inc(root_made, 1)

            def high_parts(g, slab, pos):
                arrived(act, g, slab, pos)
                for hf in range(HALVES):
                    act.wait_ge(halves, number(g, slab, pos) * HALVES + (hf + HALF_CREDIT - HIGHS + 1))
                    nc.scalar.activation(a_hi[:, (HALVES * pos + hf) % HIGHS, :],
                                         ring[:, pos % RING, hf * HALF:(hf + 1) * HALF],
                                         ACT.Copy).then_inc(hi_made, 1)

            def split_squares(slab):
                wait_alone(act, sq_ps, slab + 1)
                nc.scalar.activation(nsq[:, ds(slab * SLAB, SLAB)], bank(5), ACT.Copy)
                nc.scalar.activation(sq_col[:, ds(slab * QT, QT)], bank(6)[:, 0:QT], ACT.Copy, scale=-1.0)
                nc.scalar.activation(nsq_col[:, ds(slab * QT, QT)], bank(6)[:, 0:QT],
                                     ACT.Copy).then_inc(sq_hi_made, 1)
                wait_alone(act, sq_rest, slab + (1 + TURN))
                nc.scalar.activation(sq_mid[:, :], rest[:, :], ACT.Copy)
                nc.scalar.activation(nsq[32:64, ds(slab * SLAB, SLAB)], rest[32:64, :],
                                     ACT.Copy).then_inc(sq_mid_made, 1)

            def z_parts(slab):
                wait_alone(act, z_slab_made, slab + 1)
                nc.scalar.activation(z_hi[:, ds(slab * SLAB, SLAB)], z_slab[:, :], ACT.Copy).then_inc(z_hi_made, 1)
                nc.scalar.activation(zsq[:, :], z_slab[:, :], ACT.Square).then_inc(zsq_made, 1)

            def sweep2(g, slab, follows):
                for pos in range(sweep2_len(g)):
                    high_parts(g, slab, pos)
                    if follows and pos == 1:
                        z_parts(slab - 1)
                    if pos == QPG - 1:
                        if follows:
                            split_squares(slab - 1)
                            wait_alone(act, z_scaled, slab)
                        act.wait_ge(d_row_ps, slab + (1 + TURN))
                        nc.scalar.activation(d_row[:, :], bank(4), ACT.Copy).then_inc(d_row_made, 1)

            for g in range(GROUPS):
                sweep2(g, SPG * g, g > 0)
                with act.Fori(SPG * g + 1, SPG * (g + 1)) as slab:
                    sweep2(g, slab, True)
            z_parts(SLABS - 1)
            split_squares(SLABS - 1)

            act.wait_ge(sq_lo_made, SLABS)
            act.sem_inc(score_saved, 2)
            with act.Fori(0, TILES // 2) as pair:
                for u in range(2):
                    def negate(q):
                        act.wait_ge(score_saved, pair * (2 * QUARTERS) + (u * QUARTERS + q + 1 + 2))
                        part = rows[u][:, q * QUARTER:(q + 1) * QUARTER]
                        nc.scalar.activation(part, part, ACT.Copy, scale=-1.0).then_inc(negated, 1)

                    act.wait_ge(row_free, pair * 2 + (u + 1))
                    for q in range(QUARTERS):
                        wait_alone(act, score_ps, pair * (2 * QUARTERS) + (u * QUARTERS + q + 1))
                        odd = q % 2
                        nc.scalar.activation(rows[u][:, q * QUARTER:(q + 1) * QUARTER], bank(4 * odd, 4),
                                             ACT.Relu if odd else ACT.Identity, scale=-1.0 if odd else 1.0,
                                             bias=(sq_col if odd else nsq_col)[:, ds(pair * 2 + u, 1)]
                                             ).then_inc(score_saved, 1)
                        if q == 2:
                            negate(1)
                    negate(3)
            act.wait_ge(top_saved, 4)
            kv = kern[:, :, :].rearrange("p t k -> p (t k)")
            nc.scalar.activation(kv, v_all[:, PADT:, :].rearrange("p t k -> p (t k)"), ACT.Sqrt,
                                 bias=eps_dist[:, 0:1], scale=-1.0).then_inc(dist_made, 1)
            act.wait_ge(dist_made, 1)
            nc.scalar.activation(kv, kv, ACT.Exp, scale=-0.5).then_inc(kern_made, 1)
            act.wait_ge(sum2_made, 1)
            nc.scalar.activation(root[:, :], rowsum[:, :], ACT.Sqrt).then_inc(root2_made, 1)

            for part in range(GROUPS):
                t = slice(part * TILES // GROUPS, (part + 1) * TILES // GROUPS)
                act.wait_ge(w_made, part + 1)
                nc.scalar.activation(w_hi[:, t, :], w_all[:, t, :], ACT.Copy).then_inc(w_hi_made, 1)
                for pos in range(QPG * part, QPG * (part + 1)):
                    high_parts(None, 0, pos)

            def out_to_sbuf(slab, odd):
                products_done(act, None, slab)
                nc.scalar.activation(oT[:, :], bank(odd), ACT.Copy).then_inc(oT_made, 1)

            def last_pass(slab, odd):
                for pos in range(QUADS):
                    high_parts(None, slab, pos)
                    if pos == 1:
                        out_to_sbuf(slab - 1, 1 - odd)
                    if pos == QPG + 1:
                        act.wait_ge(oT_ps, slab)

            last_pass(1, 1)
            with act.Fori(1, SLABS // 2) as pair:
                for odd in range(2):
                    last_pass(pair * 2 + odd, odd)
            out_to_sbuf(SLABS - 1, 1)

        @block.vector
        def _(dve):
            steps = [0]
            for signal in (folded, sq_rest):
                dve.sem_inc(signal, TURN)
            dve.sem_inc(added, ADD_CREDIT)

            def step(ins):
                steps[0] += 1
                ins.then_inc(dve_step, 1)
                dve.wait_ge(dve_step, steps[0])

            def inverse_root(dst, src, rt, nt):
                step(nc.vector.reciprocal(dst, rt))
                step(nc.vector.tensor_tensor(nt, dst, dst, ALU.mult))
                step(nc.vector.tensor_tensor(nt, nt, src, ALU.mult))
                step(nc.vector.tensor_scalar(nt, nt, -0.5, 1.5, ALU.mult, ALU.add))
                step(nc.vector.tensor_tensor(dst, dst, nt, ALU.mult))

            dve.wait_ge(x_loaded, 16)
            LT = QPG * QT
            for g in range(GROUPS):
                with dve.Fori(SPG * g, SPG * (g + 1)) as slab:
                    if g == 0:
                        xq = xn[:, ds(slab * LT, LT), :]
                        nc.vector.tensor_reduce(mean[:, :], xq, AX.X, ALU.add).then_inc(ln_step, 1)
                        dve.wait_ge(ln_step, slab * 3 + 1)
                        nc.vector.tensor_scalar(mean[:, :], mean[:, :], 1.0 / D, None, ALU.mult).then_inc(ln_step, 1)
                        dve.wait_ge(ln_step, slab * 3 + 2)
                        nc.vector.tensor_tensor(xq, xq, mean[:, :].unsqueeze(2).to_broadcast([P, LT, D]),
                                                ALU.subtract).then_inc(centred, 1)
                    arrived1(dve, slab, 0)
                    arrived1(dve, slab, 1)
                    dve.wait_ge(folded, slab * 2 + TURN)
                    nc.vector.tensor_tensor(acc[:, :], ring[:, 0, :], ring[:, 1, :], ALU.add).then_inc(added, 1)
                    for pos in range(2, QUADS):
                        arrived1(dve, slab, pos)
                        dve.wait_ge(added, slab * ADDS + (ADD_CREDIT + pos - 1))
                        nc.vector.tensor_tensor(acc[:, :], acc[:, :], ring[:, pos % RING, :],
                                                ALU.add).then_inc(added, 1)
                        if g == 0 and pos == 3:
                            dve.wait_ge(squared, slab + 1)
                            nc.vector.tensor_reduce(var[:, :], square[:, :, :], AX.X, ALU.add).then_inc(var_made, 1)
                        if g == 0 and pos == 6:
                            dve.wait_ge(std_made, slab + 1)
                            nc.vector.reciprocal(var[:, :], std[:, :]).then_inc(ln_step, 1)
                            dve.wait_ge(ln_step, slab * 3 + 3)
                            nc.vector.tensor_tensor(xq, xq, var[:, :].unsqueeze(2).to_broadcast([P, LT, D]),
                                                    ALU.mult).then_inc(normed, 1)
                    dve.wait_ge(added, slab * ADDS + (ADD_CREDIT + ADDS))
                    nc.vector.tensor_tensor(half[:, :], acc[:, 0:BLOCK // 2], acc[:, BLOCK // 2:BLOCK],
                                            ALU.add).then_inc(folded, 1)
                    dve.wait_ge(folded, slab * 2 + (1 + TURN))
                    dve.wait_ge(rowsum_ps, slab + TURN)
                    nc.vector.tensor_tensor(colsum[:, :], half[:, 0:SLAB], half[:, SLAB:2 * SLAB],
                                            ALU.add).then_inc(folded, 1)
                tiles = slice(g * LT, (g + 1) * LT)
                dve.wait_ge(rowsum_ps, SPG * (g + 1) + TURN)
                nc.vector.tensor_copy(rowsum[:, tiles], row_ps[:, tiles]).then_inc(rowsum_saved, 1)
                dve.wait_ge(rowsum_saved, g + 1)
                dve.wait_ge(root_made, g + 1)
                inverse_root(deg[:, tiles], rowsum[:, tiles], root[:, tiles], newton[:, tiles])
                dve.wait_ge(hw_saved, 2 * QPG * (g + 1))
                nc.vector.tensor_tensor(hw1[:, tiles, :], hw1[:, tiles, :],
                                        deg[:, tiles].unsqueeze(2).to_broadcast([P, LT, D]),
                                        ALU.mult).then_inc(y_made, 1)
                dve.wait_ge(y_made, g + 1)
                nc.vector.tensor_copy(y_hi[:, tiles, :], hw1[:, tiles, :]).then_inc(y_hi_made, 1)
            dve.wait_ge(y_hi_made, GROUPS)
            for g in range(GROUPS):
                tiles = slice(g * LT, (g + 1) * LT)
                nc.vector.tensor_tensor(y_lo[:, tiles, :], hw1[:, tiles, :], y_hi[:, tiles, :].bitcast(f32),
                                        ALU.subtract).then_inc(y_lo_made, 1)

            def low_parts(g, slab, pos):
                for hf in range(HALVES):
                    here = slice(hf * HALF, (hf + 1) * HALF)
                    dve.wait_ge(hi_made, number(g, slab, pos) * HALVES + (hf + 1))
                    nc.vector.tensor_tensor(ring_lo[:, pos % RING, here], ring[:, pos % RING, here],
                                            a_hi[:, (HALVES * pos + hf) % HIGHS, :].bitcast(f32),
                                            ALU.subtract).then_inc(lo_made, 1)

            def split_squares(slab):
                dve.wait_ge(sq_hi_made, slab + 1)
                nc.vector.tensor_tensor(rest[:, :], bank(5), nsq[:, ds(slab * SLAB, SLAB)],
                                        ALU.subtract).then_inc(sq_rest, 1)
                dve.wait_ge(sq_mid_made, slab + 1)
                dve.wait_ge(sq_rest, slab + (1 + TURN))
                nc.vector.tensor_tensor(nsq[64:96, ds(slab * SLAB, SLAB)], rest[64:96, :], sq_mid[64:96, :],
                                        ALU.subtract).then_inc(sq_lo_made, 1)

            def z_of(g, slab):
                up = psum[:, ds((slab - SPG * g) * SLAB, SLAB)]
                dve.wait_ge(d_row_made, slab + (1 + TURN))
                products_done(dve, g, slab)
                if g:
                    nc.vector.tensor_tensor(u_sum[:, :], up, xu[:, ds(slab * SLAB, SLAB)],
                                            ALU.add).then_inc(u_step, 1)
                    dve.wait_ge(u_step, slab - (SPG - 1))
                    nc.vector.tensor_tensor(u_sum[:, :], u_sum[:, :], d_row[:, :], ALU.mult).then_inc(z_scaled, 1)
                else:
                    nc.vector.tensor_tensor(u_sum[:, :], up, d_row[:, :], ALU.mult).then_inc(z_scaled, 1)
                dve.wait_ge(z_scaled, slab + 1)
                nc.vector.tensor_scalar(u_sum[:, :], u_sum[:, :], b1c[:, 0:1], None, ALU.add).then_inc(z_shifted, 1)
                dve.wait_ge(z_shifted, slab + 1)
                nc.vector.scalar_tensor_tensor(z_slab[:, :], u_sum[:, :], SLOPE, u_sum[:, :], ALU.mult,
                                               ALU.max).then_inc(z_slab_made, 1)

            def z_low(slab):
                dve.wait_ge(z_hi_made, slab + 1)
                nc.vector.tensor_tensor(z_lo[:, ds(slab * SLAB, SLAB)], z_slab[:, :],
                                        z_hi[:, ds(slab * SLAB, SLAB)].bitcast(f32),
                                        ALU.subtract).then_inc(z_made, 1)

            def sweep2(g, slab, before):
                for pos in range(sweep2_len(g)):
                    low_parts(g, slab, pos)
                    if before is not None:
                        if pos == 0:
                            z_of(before, slab - 1)
                        elif pos == 1:
                            z_low(slab - 1)
                        elif pos == QPG - 1:
                            split_squares(slab - 1)

            dve.wait_ge(partial_saved, (GROUPS - 1) * SPG)
            for g in range(GROUPS):
                sweep2(g, SPG * g, g - 1 if g else None)
                with dve.Fori(SPG * g + 1, SPG * (g + 1)) as slab:
                    sweep2(g, slab, g)
            z_of(GROUPS - 1, SLABS - 1)
            z_low(SLABS - 1)
            split_squares(SLABS - 1)

            dve.wait_ge(sq_lo_made, SLABS)
            dve.wait_ge(tops_clear, 4)
            dve.sem_inc(row_free, 2)
            with dve.Fori(0, TILES // 2) as pair:
                for u in range(2):
                    dve.wait_ge(negated, pair * QUARTERS + (u + 1) * (QUARTERS // 2))
                    wait_alone(dve, clamped, pair * QUARTERS + (u + 1) * (QUARTERS // 2))
                    nc.vector.max(top_v[u][:, :], rows[u][:, :]).then_inc(max_found, 1)
                    wait_alone(dve, max_found, pair * 2 + (u + 1))
                    nc.vector.max_index(top_i[u][:, :], top_v[u][:, :], rows[u][:, :]).then_inc(row_free, 1)

            dve.wait_ge(kern_made, 1)
            step(nc.vector.tensor_reduce(near_sum[:, :], kern[:, :, :], AX.X, ALU.add))
            nc.vector.tensor_tensor(rowsum[:, :], rowsum[:, :], near_sum[:, :], ALU.add).then_inc(sum2_made, 1)
            dve.wait_ge(sum2_made, 1)
            dve.wait_ge(root2_made, 1)
            inverse_root(deg2[:, :], rowsum[:, :], root[:, :], newton[:, :])
            dve.wait_ge(hw2_loaded, 16)

            def scale_w(part):
                t = slice(part * TILES // GROUPS, (part + 1) * TILES // GROUPS)
                nc.vector.tensor_tensor(w_all[:, t, :], w_all[:, t, :],
                                        deg2[:, t].unsqueeze(2).to_broadcast([P, TILES // GROUPS, D]),
                                        ALU.mult).then_inc(w_made, 1)

            def neighbour(slab, c):
                if c == 0:
                    dve.wait_ge(gathered, slab * (16 * GATHERS) + 16 * GATHERS)
                rows_c = gat[:, c * TOPK * D:(c + 1) * TOPK * D]
                g3 = rows_c.rearrange("p (k d) -> p k d", d=D)
                weights = kern[:, ds(slab * QT + c, 1), :].rearrange("p t k -> p (t k)")
                nc.vector.tensor_tensor(g3, g3, weights.unsqueeze(2).to_broadcast([P, TOPK, D]),
                                        ALU.mult).then_inc(near_step, 1)
                wait_alone(dve, near_step, slab * QT + (c + 1))
                nc.vector.tensor_reduce(near[:, c * D:(c + 1) * D], rows_c.rearrange("p (k d) -> p d k", d=D),
                                        AX.X, ALU.add).then_inc(near_made, 1)

            def output(slab, stage):
                m3 = mix[:, :].rearrange("p (c d) -> p c d", d=D)
                if stage == 0:
                    dve.wait_ge(near_made, slab * QT + QT)
                    dve.wait_ge(oT_ps, slab + 1)
                    nc.vector.tensor_tensor(mix[:, :], bank(4), near[:, :], ALU.add).then_inc(mix_step, 1)
                elif stage == 1:
                    wait_alone(dve, mix_step, slab * 3 + 1)
                    nc.vector.tensor_tensor(m3, m3, deg2[:, ds(slab * QT, QT)].unsqueeze(2).to_broadcast([P, QT, D]),
                                            ALU.mult).then_inc(mix_step, 1)
                elif stage == 2:
                    dve.wait_ge(mix_step, slab * 3 + 2)
                    nc.vector.tensor_tensor(m3, m3, b2all[:, :].unsqueeze(1).to_broadcast([P, QT, D]),
                                            ALU.add).then_inc(mix_step, 1)
                else:
                    dve.wait_ge(mix_step, slab * 3 + 3)
                    dve.wait_ge(xs_loaded, slab * 16 + 16)
                    nc.vector.tensor_tensor(outs[:, :], mix[:, :], xs[:, :], ALU.add).then_inc(outs_made, 1)

            scale_w(0)
            scale_w(1)
            for part in range(GROUPS):
                t = slice(part * TILES // GROUPS, (part + 1) * TILES // GROUPS)
                dve.wait_ge(w_hi_made, part + 1)
                nc.vector.tensor_tensor(w_lo[:, t, :], w_all[:, t, :], w_hi[:, t, :].bitcast(f32),
                                        ALU.subtract).then_inc(w_lo_made, 1)
                for pos in range(QPG * part, QPG * (part + 1)):
                    low_parts(None, 0, pos)
                if part + 2 < GROUPS:
                    scale_w(part + 2)

            def last_pass(slab):
                for pos in range(QUADS):
                    low_parts(None, slab, pos)
                    if 2 <= pos < 2 + QT:
                        neighbour(slab - 1, pos - 2)
                    if QUADS // 2 <= pos < QUADS // 2 + 4:
                        output(slab - 1, pos - QUADS // 2)

            last_pass(1)
            with dve.Fori(1, SLABS // 2) as pair:
                for odd in range(2):
                    last_pass(pair * 2 + odd)
            for c in range(QT):
                neighbour(SLABS - 1, c)
            for stage in range(4):
                output(SLABS - 1, stage)

        @block.tensor
        def _(pe):
            for signal in (rowsum_ps, d_row_ps):
                pe.sem_inc(signal, TURN)
            pe.wait_ge(const_made, CONSTANTS)
            pe.wait_ge(small_loaded, 64)
            nc.tensor.matmul(bank(4)[:, 0:D], ones[:, :], b2row[:, :], start=True, stop=True).then_inc(b2_ps, 1)
            pe.wait_ge(b2_made, 1)
            pe.sem_inc(multiplied, MULT_CREDIT)
            pe.sem_inc(halves, HALF_CREDIT)

            def prepare(b):
                pe.wait_ge(h_made, b + 1)
                for c in range(QT):
                    ins = nc.tensor.transpose(bank(4)[:, c * P:(c + 1) * P], hs[:, c, :], ident[:, :])
                ins.then_inc(hT_ps, 1)
                pe.wait_ge(hT_made, b + 1)
                for c in range(QT):
                    ins = nc.tensor.matmul(bank(5, 2)[:, c * 2 * D:(c + 1) * 2 * D], hT[:, c * P:(c + 1) * P],
                                           w12[:, :, :].rearrange("p w d -> p (w d)"), start=True, stop=True)
                ins.then_inc(hw_ps, 1)

            def product(dst, q, slot, first, last):
                for c in range(QT):
                    ins = nc.tensor.matmul(dst, hw1[:, q * QT + c, :], ring[:, slot, c * SLAB:(c + 1) * SLAB],
                                           start=first and c == 0, stop=last and c == QT - 1)
                ins.then_inc(multiplied, 1)

            for g in range(GROUPS):
                if g:
                    pe.wait_ge(y_made, g)
                if g > 1:
                    pe.wait_ge(partial_saved, SPG * (g - 1))
                with pe.Fori(SPG * g, SPG * (g + 1)) as slab:
                    if g == 0:
                        for j in range(SPG):
                            prepare(slab * SPG + j)
                    dst = psum[:, ds((slab - SPG * g) * SLAB, SLAB)]
                    for pos, (q, mult) in enumerate(order1(g)):
                        if mult:
                            arrived1(pe, slab, pos)
                            product(dst, q, pos % RING, q == 0, q == QPG * g - 1)
                    pe.wait_ge(folded, slab * 2 + (2 + TURN))
                    for c in range(QT):
                        ins = nc.tensor.matmul(row_ps[:, ds(slab * QT + c, 1)], colsum[:, c * P:(c + 1) * P],
                                               ones[:, 0:1], start=True, stop=True)
                    ins.then_inc(rowsum_ps, 1)

            def split_product(dst, v_hi, v_lo, g, slab, pos, first, last):
                q = (QPG * g if g else 0) + pos
                for hf in range(HALVES):
                    turn = number(g, slab, pos) * HALVES + (hf + 1)
                    pe.wait_ge(hi_made, turn)
                    for c in range(QT // HALVES):
                        t = q * QT + hf * (QT // HALVES) + c
                        cols = a_hi[:, (HALVES * pos + hf) % HIGHS, c * SLAB:(c + 1) * SLAB]
                        nc.tensor.matmul(dst, v_hi[:, t, :], cols, start=first and hf == 0 and c == 0, stop=False)
                        nc.tensor.matmul(dst, v_lo[:, t, :], cols, start=False, stop=False)
                    pe.wait_ge(lo_made, turn)
                    for c in range(QT // HALVES):
                        t = q * QT + hf * (QT // HALVES) + c
                        i = hf * HALF + c * SLAB
                        ins = nc.tensor.matmul(dst, v_hi[:, t, :], ring_lo[:, pos % RING, i:i + SLAB], start=False,
                                               stop=last and hf == HALVES - 1 and c == QT // HALVES - 1)
                    ins.then_inc(halves, 1)

            def squares(slab):
                pe.wait_ge(zsq_made, slab + 1)
                pe.wait_ge(sq_rest, slab + TURN)
                nc.tensor.matmul(bank(5), neg_ones[:, :], zsq[:, :], start=True, stop=True)
                for c in range(QT):
                    ins = nc.tensor.matmul(bank(6)[:, c:c + 1], zsq[:, c * P:(c + 1) * P], neg_ones[:, 0:1],
                                           start=True, stop=True)
                ins.then_inc(sq_ps, 1)

            def sweep2(g, slab):
                n = sweep2_len(g)
                dst = psum[:, ds((slab - SPG * g) * SLAB, SLAB)]
                if g:
                    pe.wait_ge(z_scaled, slab - (SPG - 1))
                for pos in range(n):
                    split_product(dst, y_hi, y_lo, g, slab, pos, pos == 0, pos == n - 1)
                    if pos == QPG - 1:
                        if g or not isinstance(slab, int):
                            squares(slab - 1)
                        pe.wait_ge(diag_made, slab + 1)
                        pe.wait_ge(d_row_made, slab + TURN)
                        nc.tensor.matmul(bank(4), ones[:, :], diag[:, :], start=True, stop=True).then_inc(d_row_ps, 1)

            pe.wait_ge(partial_saved, SPG * (GROUPS - 1))
            for part in range(GROUPS):
                pe.wait_ge(y_lo_made, part + 1)
            for g in range(GROUPS):
                sweep2(g, SPG * g)
                with pe.Fori(SPG * g + 1, SPG * (g + 1)) as slab:
                    sweep2(g, slab)
            squares(SLABS - 1)

            with pe.Fori(0, TILES // 2) as pair:
                for u in range(2):
                    pe.wait_ge(z2_made, pair * 4 + (u + 1) * 2)
                    for q in range(QUARTERS):
                        pe.wait_ge(score_saved, pair * (2 * QUARTERS) + (u * QUARTERS + q + 1))
                        cols = [slice(j, j + SLAB) for j in range(q * QUARTER, (q + 1) * QUARTER, SLAB)]
                        for c, j in enumerate(cols):
                            nc.tensor.matmul(bank(4 * (q % 2) + c), z2_hi[:, u, :], z_hi[:, j], start=True, stop=False)
                            nc.tensor.matmul(bank(4 * (q % 2) + c), z2_hi[:, u, :], z_lo[:, j], start=False, stop=False)
                        for c, j in enumerate(cols):
                            nc.tensor.matmul(bank(4 * (q % 2) + c), z2_lo[:, u, :], z_hi[:, j], start=False, stop=False)
                        for c, j in enumerate(cols):
                            ins = nc.tensor.matmul(bank(4 * (q % 2) + c), part_rows[:, :],
                                                   nsq[:, j], start=False, stop=True)
                        ins.then_inc(score_ps, 1)

            def transposes(slab, first=False):
                pe.wait_ge(oT_made, slab + 1)
                if not first:
                    pe.wait_ge(outs_made, slab)
                for c in range(QT):
                    ins = nc.tensor.transpose(bank(4)[:, c * P:(c + 1) * P], oT[:, c * P:(c + 1) * P], ident[:, :])
                ins.then_inc(oT_ps, 1)

            def last_pass(slab, odd, first=False):
                for pos in range(QUADS):
                    split_product(bank(odd), w_hi, w_lo, None, slab, pos, pos == 0, pos == QUADS - 1)
                    if pos == QPG - 1:
                        transposes(slab - 1, first)

            pe.wait_ge(score_saved, 2 + TILES * QUARTERS)
            for pos in range(QUADS):
                if pos % QPG == 0:
                    pe.wait_ge(w_lo_made, pos // QPG + 1)
                split_product(bank(0), w_hi, w_lo, None, 0, pos, pos == 0, pos == QUADS - 1)
            last_pass(1, 1, True)
            with pe.Fori(1, SLABS // 2) as pair:
                for odd in range(2):
                    last_pass(pair * 2 + odd, odd)
            transposes(SLABS - 1)


def kernel(x, adj, L0_gnn_W1, L0_gnn_b1, L0_gnn_W2, L0_gnn_b2):
    import concourse.bacc as bacc
    from concourse.bass_utils import run_bass_kernel_spmd

    at = np.asarray(adj).T.reshape(QUADS, QT, P, SLABS, SLAB)
    at = np.ascontiguousarray(at.transpose(3, 0, 2, 1, 4)).reshape(SLABS, QUADS, P, BLOCK)
    arrays = {
        "x": np.ascontiguousarray(x), "at_blocks": at,
        "w1": np.ascontiguousarray(L0_gnn_W1), "b1": np.ascontiguousarray(L0_gnn_b1),
        "w2": np.ascontiguousarray(L0_gnn_W2), "b2": np.ascontiguousarray(L0_gnn_b2),
    }
    nc = bacc.Bacc("TRN2", target_bir_lowering=False, num_devices=1, dynamic_dma_scratch_size=8192)
    f32 = mybir.dt.float32
    aps = {k: nc.dram_tensor(k, list(a.shape), f32, kind="ExternalInput").ap() for k, a in arrays.items()}
    out = nc.dram_tensor("out", [N, D], f32, kind="ExternalOutput").ap()
    w_table = nc.dram_tensor("w_table", [N, D], f32, kind="Internal").ap()
    hw2_table = nc.dram_tensor("hw2_table", [N, D], f32, kind="Internal").ap()
    build(nc, **aps, out=out, w_table=w_table, hw2_table=hw2_table)
    r = run_bass_kernel_spmd(nc, [arrays], core_ids=[0])
    return r.results[0]["out"]
```

```python
from contextlib import ExitStack

import concourse.bass as bass
import concourse.mybir as mybir
import numpy as np

P = 128
N = 8192
D = 128
TILES = N // P
SLAB = 512
SLABS = N // SLAB
QT = SLAB // P
QUADS = TILES // QT
GROUPS = 8
SPG = SLABS // GROUPS
QPG = QUADS // GROUPS
PREPS = 4
PREP_SLABS = PREPS
PREP_TILES = TILES // PREPS
BATCHES = QUADS // PREPS
PARTS = 4
PART_QUADS = QUADS // PARTS
PART_TILES = TILES // PARTS
RING = 4
BLOCK = QT * SLAB
HALVES = 2
HALF = BLOCK // HALVES
HIGHS = 4
TOPK = 4
PADT = 2
CHUNKS = (((4, False, True), (3, True, False), (4, False, True), (3, True, False), (2, False, False)),
          ((3, True, True), (4, False, True), (3, True, False), (4, False, False), (2, True, False)))
NCHUNKS = len(CHUNKS[0])
CLAMPS = 2
assert all(sum(c[0] for c in cs) == SLABS and sum(c[2] for c in cs) == CLAMPS for cs in CHUNKS)
EARLY = PART_TILES + 4
EARLY_SLABS = (TILES - EARLY) // QT
LAST_QUADS = QUADS - PART_QUADS
EPS_LN = 1e-5
EPS_DIST = 1e-10
SLOPE = 0.1


def build(nc, x, at_blocks, w1, b1, w2, b2, out, w_table, hw2_table, partials):
    f32, f32r, bf16, u32 = mybir.dt.float32, mybir.dt.float32r, mybir.dt.bfloat16, mybir.dt.uint32
    ALU = mybir.AluOpType
    ACT = mybir.ActivationFunctionType
    AX = mybir.AxisListType
    ds = bass.ds

    x_tiles = x.rearrange("(t p) d -> p t d", p=P)
    out_tiles = out.rearrange("(t p) d -> p t d", p=P)
    hw2_tiles = hw2_table.rearrange("(t p) d -> p t d", p=P)
    w_tiles = w_table.rearrange("(t p) d -> p t d", p=P)

    def known(g):
        return QPG * g

    def order1(g):
        n = known(g)
        at_pos = [QUADS - 2 * (n - i) + 1 if g == 1 else (i + 1) * QUADS // n - 1 for i in range(n)]
        others = iter(range(n, QUADS))
        return [(at_pos.index(pos), True) if pos in at_pos else (next(others), False) for pos in range(QUADS)]

    def mults_through(g, pos):
        return sum(mult for _, mult in order1(g)[:pos + 1])

    def mults_before(g):
        return sum(SPG * known(i) for i in range(g))

    MULTS1 = mults_before(GROUPS)
    READS1 = SLABS * QUADS
    blocks2 = [(slab, q) for slab in range(SLABS) for q in range(known(slab // SPG), QUADS)]
    start2 = [[b[0] for b in blocks2].index(slab) for slab in range(SLABS)] + [len(blocks2)]
    READS2 = len(blocks2)
    READS3 = SLABS * PART_QUADS
    assert READS1 % RING == 0 and READS2 % RING == 0 and PART_QUADS == RING == QT
    ADDS = QUADS - 1
    GATHERS = QT * TOPK
    CONSTANTS = 12
    ADD_CREDIT = RING
    MULT_CREDIT = RING
    HALF_CREDIT = HALVES * RING
    TURN = 1

    ctx = ExitStack()
    with ctx:
        def sem(name):
            return ctx.enter_context(nc.semaphore(name))

        place = [-(-nc.sbuf_base // 32) * 32]

        def room(nbytes):
            place[0] += nbytes
            return place[0] - nbytes

        def at(offset, name, shape, dt=f32):
            return nc.alloc_sbuf_tensor_at(name, shape, dt, offset=offset)

        def sb(name, shape, dt=f32):
            size = int(np.prod(shape[1:])) * {f32: 4, f32r: 4, u32: 4, bf16: 2}[dt]
            return at(room(-(-size // 32) * 32), name, shape, dt)

        r1 = room(4 * (N + PADT * P))
        xu = at(r1, "xu", [P, N])
        z_hi = at(r1, "z_hi", [P, N + PADT * P], f32r)
        w_hi = at(r1, "w_hi", [P, TILES, D], f32r)
        r2 = room(4 * (N + PADT * P))
        acc = at(r2, "acc", [P, BLOCK])
        half = at(r2 + 8192, "half", [P, BLOCK // 2])
        colsum = at(r2 + 12288, "colsum", [P, SLAB])
        hs = at(r2 + 14336, "hs", [P, QT, D])
        hT = at(r2 + 16384, "hT", [P, QT * P])
        square = at(r2 + 18432, "square", [P, PREP_TILES, D])
        hw2_out = at(r2 + 18432, "hw2_out", [P, PREP_TILES, D])
        z_lo = at(r2, "z_lo", [P, N + PADT * P], f32r)
        w_lo = at(r2, "w_lo", [P, TILES, D], f32r)
        r3 = room(4 * N)
        hw1 = at(r3, "hw1", [P, TILES, D])
        y_lo = at(r3, "y_lo", [P, TILES, D], f32r)
        row0 = at(r3, "row0", [P, N])
        w_all = at(r3, "w_all", [P, TILES, D])
        r4 = room(4 * N)
        y_hi = at(r4, "y_hi", [P, TILES, D], f32r)
        row1 = at(r4, "row1", [P, N])
        gat = at(r4, "gat", [P, QT * TOPK * D])
        near = at(r4 + 8192, "near", [P, QT * D])
        oT = at(r4 + 10240, "oT", [P, SLAB])
        xs = at(r4 + 12288, "xs", [P, QT * D])
        mix = at(r4 + 14336, "mix", [P, QT * D])
        outs = at(r4 + 16384, "outs", [P, QT * D])
        part_in = at(r4 + 18432, "part_in", [P, SLAB])
        part_late = at(r4 + 20480, "part_late", [P, (SLABS - EARLY_SLABS) * SLAB])
        rows = [row0, row1]
        r5 = room(4 * RING * BLOCK)
        ring = at(r5, "ring", [P, RING, BLOCK])
        ring_lo = at(r5, "ring_lo", [P, RING, BLOCK], f32r)
        ra = room(4 * HIGHS * HALF)
        a_hi = at(ra, "a_hi", [P, HIGHS, HALF], f32r)
        w_first = at(ra, "w_first", [P, PART_TILES, D])
        part_out = at(ra + 8192, "part_out", [P, SLAB])
        nsq = sb("nsq", [P, N], bf16)
        r6 = room(6 * 4 * SLAB)
        diag = at(r6, "diag", [P, SLAB])
        d_row = at(r6 + 2048, "d_row", [P, SLAB])
        u_sum = at(r6 + 4096, "u_sum", [P, SLAB])
        z_slab = at(r6 + 6144, "z_slab", [P, SLAB])
        zsq = at(r6 + 8192, "zsq", [P, SLAB])
        rest = at(r6 + 10240, "rest", [P, SLAB])
        z2_hi = at(r6, "z2_hi", [P, 2, P], f32r)
        z2_lo = at(r6 + 1024, "z2_lo", [P, 2, P], f32r)
        v_all = at(r6 + 2048, "v_all", [P, PADT + TILES, TOPK])
        i_all = at(r6 + 3584, "i_all", [P, PADT + TILES, TOPK], u32)
        kern = at(r6 + 5120, "kern", [P, TILES, TOPK])
        gather_i = at(r6 + 6144, "gather_i", [P, QT * TOPK], u32)
        top_v = [at(r6 + 6272 + 32 * u, f"top_v{u}", [P, 8]) for u in range(2)]
        top_i = [at(r6 + 6336 + 32 * u, f"top_i{u}", [P, 8], u32) for u in range(2)]
        sq_mid = sb("sq_mid", [P, SLAB], bf16)
        ident = sb("ident", [P, P])
        ones = sb("ones", [P, P])
        neg_ones = sb("neg_ones", [P, P])
        part_rows = sb("part_rows", [P, P], bf16)
        w12 = sb("w12", [P, 2, D])
        b1c = sb("b1c", [P, 1])
        b2row = sb("b2row", [P, D])
        b2all = sb("b2all", [P, D])
        eps_ln = sb("eps_ln", [P, 1])
        eps_dist = sb("eps_dist", [P, 1])
        mean = sb("mean", [P, PREP_TILES])
        var = sb("var", [P, PREP_TILES])
        std = sb("std", [P, PREP_TILES])
        rowsum = sb("rowsum", [P, TILES])
        root = sb("root", [P, TILES])
        newton = sb("newton", [P, TILES])
        inverse = sb("inverse", [P, TILES])
        deg = sb("deg", [P, TILES])
        deg2 = sb("deg2", [P, TILES])
        near_sum = sb("near_sum", [P, TILES])
        nsq_col = sb("nsq_col", [P, TILES])
        sq_col = sb("sq_col", [P, TILES])
        assert place[0] <= nc.sbuf_usable_end
        xn = xu[:, :].rearrange("p (t d) -> p t d", d=D)

        psum = ctx.enter_context(nc.psum_tensor("psum", [P, 8 * SLAB], f32))

        def bank(i, n=1):
            return psum[:, i * SLAB:(i + n) * SLAB]

        row_ps = bank(7)[:, 0:TILES]

        const_made = sem("const_made")
        row0_clear = sem("row0_clear")
        small_loaded = sem("small_loaded")
        x_loaded = sem("x_loaded")
        block_loaded = [sem(f"block_loaded{i}") for i in range(RING)]
        added = sem("added")
        multiplied = sem("multiplied")
        hi_made = sem("hi_made")
        lo_made = sem("lo_made")
        halves = sem("halves")
        dve_step = sem("dve_step")
        ln_step = sem("ln_step")
        centred = sem("centred")
        squared = sem("squared")
        var_made = sem("var_made")
        std_made = sem("std_made")
        normed = sem("normed")
        b2_ps = sem("b2_ps")
        b2_made = sem("b2_made")
        h_made = sem("h_made")
        hT_ps = sem("hT_ps")
        hT_made = sem("hT_made")
        hw_ps = sem("hw_ps")
        hw_saved = sem("hw_saved")
        hw2_stored = sem("hw2_stored")
        hw2_loaded = sem("hw2_loaded")
        folded = sem("folded")
        rowsum_ps = sem("rowsum_ps")
        rowsum_saved = sem("rowsum_saved")
        root_made = sem("root_made")
        newton_step = sem("newton_step")
        y_made = sem("y_made")
        y_hi_made = sem("y_hi_made")
        y_lo_made = sem("y_lo_made")
        partial_saved = sem("partial_saved")
        diag_made = sem("diag_made")
        d_row_ps = sem("d_row_ps")
        d_row_made = sem("d_row_made")
        u_step = sem("u_step")
        z_scaled = sem("z_scaled")
        z_shifted = sem("z_shifted")
        z_slab_made = sem("z_slab_made")
        zsq_made = sem("zsq_made")
        z_hi_made = sem("z_hi_made")
        z_made = sem("z_made")
        sq_ps = sem("sq_ps")
        sq_hi_made = sem("sq_hi_made")
        sq_rest = sem("sq_rest")
        sq_mid_made = sem("sq_mid_made")
        sq_lo_made = sem("sq_lo_made")
        tops_clear = sem("tops_clear")
        z2_made = sem("z2_made")
        score_ps = sem("score_ps")
        score_saved = sem("score_saved")
        clamped = sem("clamped")
        negated = sem("negated")
        max_found = sem("max_found")
        row_free = sem("row_free")
        top_saved = sem("top_saved")
        dist_made = sem("dist_made")
        kern_made = sem("kern_made")
        sum2_made = sem("sum2_made")
        root2_made = sem("root2_made")
        w_made = sem("w_made")
        w_hi_made = sem("w_hi_made")
        w_lo_made = sem("w_lo_made")
        w_stored = sem("w_stored")
        gather_i_made = sem("gather_i_made")
        gathered = sem("gathered")
        near_step = sem("near_step")
        near_made = sem("near_made")
        part_saved = sem("part_saved")
        part_stored = sem("part_stored")
        part_loaded = sem("part_loaded")
        oT_made = sem("oT_made")
        oT_ps = sem("oT_ps")
        xs_loaded = sem("xs_loaded")
        mix_step = sem("mix_step")
        outs_made = sem("outs_made")
        out_stored = sem("out_stored")
        waits_passed = sem("waits_passed")

        def wait_alone(eng, signal, value):
            eng.wait_ge(signal, value)
            eng.sem_inc(waits_passed, 1)

        def split2(k):
            return k, 16 * ((READS1 + k) // RING + 1), k % RING, k

        def early(slab, pos):
            return (slab * PART_QUADS + (READS2 + pos),
                    slab * (16 * PART_QUADS // RING) + 16 * ((READS1 + READS2 + pos) // RING + 1), pos % RING)

        def split3(slab, pos):
            return (slab * LAST_QUADS + (READS2 + READS3 + pos),
                    slab * (16 * LAST_QUADS // RING) + 16 * ((READS1 + READS2 + READS3 + pos) // RING + 1),
                    pos % RING, slab * LAST_QUADS + (READS2 + pos))

        def arrived(eng, this):
            eng.wait_ge(block_loaded[this[2]], this[1])

        def arrived1(eng, slab, pos):
            eng.wait_ge(block_loaded[pos % RING], slab * (16 * QUADS // RING) + 16 * (pos // RING + 1))

        def products_done(eng, count):
            eng.wait_ge(halves, count * HALVES + HALF_CREDIT)

        def each_tile(eng, tile):
            with eng.Fori(0, PART_TILES // 2 + 1) as pair:
                for u in range(2):
                    tile(lambda k, c=0, u=u: pair * (2 * k) + (u * k + c), u)
            for t in range(PART_TILES + 2, EARLY):
                tile(lambda k, c=0, t=t: t * k + c, t % 2, single=t)
            with eng.Fori(0, EARLY_SLABS) as slab:
                for q in range(QT):
                    tile(lambda k, c=0, q=q: slab * (QT * k) + ((EARLY + q) * k + c), q % 2, slab=slab, q=q)

        block = ctx.enter_context(nc.Block())

        @block.sync
        def _(sp):
            sp.dma_start(xn[:, 0:PREP_TILES, :], x_tiles[:, 0:PREP_TILES, :]).then_inc(x_loaded, 16)
            sp.dma_start(w12[:, 0, :], w1).then_inc(small_loaded, 16)
            sp.dma_start(w12[:, 1, :], w2).then_inc(small_loaded, 16)
            sp.dma_start(b1c[:, :], b1.rearrange("(p a) -> p a", a=1)).then_inc(small_loaded, 16)
            sp.wait_ge(row0_clear, 1)
            sp.dma_start(b2row[0:1, :], b2.rearrange("(a d) -> a d", a=1)).then_inc(small_loaded, 16)

            def load(slab, q, slot):
                sp.dma_start(ring[:, slot, :], at_blocks[slab, q, :, :]).then_inc(block_loaded[slot], 16)

            for g in range(GROUPS):
                with sp.Fori(SPG * g, SPG * (g + 1)) as slab:
                    for pos in range(QUADS):
                        if pos < RING:
                            wait_alone(sp, added, slab * ADDS + (ADD_CREDIT + pos - 3))
                        else:
                            wait_alone(sp, added, slab * ADDS + (ADD_CREDIT + max(pos - RING, 1)))
                        if g and pos < RING:
                            later, later_before = (known(h) - mults_through(h, pos + QUADS - RING)
                                                   for h in (g, g - 1))
                            wait_alone(sp, multiplied, (slab - SPG * g) * (known(g) - later + later_before)
                                       + (MULT_CREDIT + mults_before(g) - later_before))
                        elif g and order1(g)[pos - RING][1]:
                            wait_alone(sp, multiplied, (slab - SPG * g) * known(g)
                                       + (MULT_CREDIT + mults_before(g) + mults_through(g, pos - RING)))
                        load(slab, order1(g)[pos][0], pos % RING)

            def slot_free(this):
                wait_alone(sp, halves, this[0] * HALVES + (HALF_CREDIT - HALVES * (RING - 1)))

            sp.wait_ge(added, ADD_CREDIT + SLABS * ADDS)
            for k, (slab, q) in enumerate(blocks2):
                if k < RING:
                    sp.wait_ge(multiplied, MULT_CREDIT + MULTS1 - known(GROUPS - 1)
                               + mults_through(GROUPS - 1, k + QUADS - RING))
                else:
                    sp.wait_ge(halves, (k - RING + 1) * HALVES + HALF_CREDIT)
                load(slab, q, k % RING)

            def reload(slab, pos):
                slot_free(split3(slab, pos))
                load(slab, PART_QUADS + pos, pos % RING)

            def load_early(slab):
                for pos in range(PART_QUADS):
                    slot_free(early(slab, pos))
                    load(slab, pos, pos)

            def store_w(part):
                sp.wait_ge(w_made, part + 1)
                t = slice(part * PART_TILES, (part + 1) * PART_TILES)
                sp.dma_start(w_tiles[:, t, :], w_all[:, t, :] if part else w_first[:, :, :]).then_inc(w_stored, 16)

            def load_x(slab):
                sp.dma_start(xs[:, :].rearrange("p (c d) -> p c d", d=D),
                             x_tiles[:, ds(slab * QT, QT), :]).then_inc(xs_loaded, 16)

            def store_out(slab):
                sp.dma_start(out_tiles[:, ds(slab * QT, QT), :],
                             outs[:, :].rearrange("p (c d) -> p c d", d=D)).then_inc(out_stored, 16)

            def load_part(slab):
                sp.dma_start(part_in[:, :], partials[:, ds(slab * SLAB, SLAB)]).then_inc(part_loaded, 16)

            def store_part(slab):
                wait_alone(sp, part_saved, slab + (1 + TURN))
                sp.dma_start(partials[:, ds(slab * SLAB, SLAB)], part_out[:, :]).then_inc(part_stored, 16)

            load_early(0)
            sp.wait_ge(hw2_stored, 16 * PREPS)
            sp.dma_start(w_first[:, :, :], hw2_tiles[:, 0:PART_TILES, :]).then_inc(hw2_loaded, 16)
            store_w(0)
            with sp.Fori(1, EARLY_SLABS + 1) as slab:
                load_early(slab)
                store_part(slab - 1)
            sp.wait_ge(row_free, 2 + TILES - 1)
            for part in range(1, PARTS):
                t = slice(part * PART_TILES, (part + 1) * PART_TILES)
                if part == PARTS - 1:
                    load_early(EARLY_SLABS + 1)
                sp.dma_start(w_all[:, t, :], hw2_tiles[:, t, :]).then_inc(hw2_loaded, 16)
            with sp.Fori(EARLY_SLABS + 2, SLABS - 1) as slab:
                load_early(slab)
            for part in range(1, PARTS):
                store_w(part)
            load_early(SLABS - 1)
            for pos in range(LAST_QUADS):
                reload(0, pos)
                if pos == RING:
                    sp.wait_ge(part_saved, SLABS + TURN)
                    sp.dma_start(partials[:, EARLY_SLABS * SLAB:], part_late[:, :]).then_inc(part_stored, 16)
            sp.wait_ge(part_stored, 16 * (EARLY_SLABS + 1 + TURN))
            load_part(0)
            for pos in range(LAST_QUADS):
                reload(1, pos)
                if pos == PART_QUADS:
                    load_x(0)
                if pos == PART_QUADS + 3:
                    sp.wait_ge(oT_ps, 1)
                    load_part(1)
            with sp.Fori(2, SLABS) as slab:
                for pos in range(LAST_QUADS):
                    reload(slab, pos)
                    if pos == PART_QUADS:
                        wait_alone(sp, outs_made, slab - 1)
                        store_out(slab - 2)
                    if pos == PART_QUADS + 2:
                        wait_alone(sp, out_stored, (slab - 1) * 16)
                        load_x(slab - 1)
                    if pos == PART_QUADS + 3:
                        wait_alone(sp, oT_ps, slab)
                        load_part(slab)
            sp.wait_ge(outs_made, SLABS - 1)
            store_out(SLABS - 2)
            sp.wait_ge(out_stored, 16 * (SLABS - 1))
            load_x(SLABS - 1)
            sp.wait_ge(outs_made, SLABS)
            store_out(SLABS - 1)
            sp.wait_ge(w_stored, 16 * PARTS)
            sp.wait_ge(out_stored, 16 * SLABS)

        @block.gpsimd
        def _(pool):
            nc.gpsimd.memset(b2row[:, :], 0.0).then_inc(row0_clear, 1)
            made = [0]

            def constant(ins):
                made[0] += 1
                ins.then_inc(const_made, 1)
                pool.wait_ge(const_made, made[0])

            constant(nc.gpsimd.memset(ident[:, :], 0.0))
            constant(nc.gpsimd.affine_select(out=ident[:, :], in_=ident[:, :], compare_op=ALU.not_equal, fill=1.0,
                                             base=0, pattern=[[-1, P]], channel_multiplier=1))
            constant(nc.gpsimd.memset(ones[:, :], 1.0))
            constant(nc.gpsimd.memset(neg_ones[:, :], -1.0))
            constant(nc.gpsimd.memset(eps_ln[:, :], EPS_LN))
            constant(nc.gpsimd.memset(eps_dist[:, :], EPS_DIST))
            constant(nc.gpsimd.memset(part_rows[:, :], 0.0))
            for r in (0, 32, 64):
                constant(nc.gpsimd.memset(part_rows[r:r + 1, :], 1.0))
            constant(nc.gpsimd.memset(z_hi[:, N:N + PADT * P].bitcast(f32), 0.0))
            constant(nc.gpsimd.memset(z_lo[:, N:N + PADT * P].bitcast(f32), 0.0))
            assert made[0] == CONSTANTS

            with pool.Fori(0, SLABS) as slab:
                wait_alone(pool, y_made, slab + 1)
                wait_alone(pool, d_row_ps, slab + TURN)
                nc.gpsimd.tensor_tensor(diag[:, :].rearrange("p (c i) -> p c i", c=QT),
                                        ident[:, :].unsqueeze(1).to_broadcast([P, QT, P]),
                                        deg[:, ds(slab * QT, QT)].unsqueeze(2).to_broadcast([P, QT, P]),
                                        ALU.mult).then_inc(diag_made, 1)

            pool.wait_ge(d_row_ps, SLABS + TURN)
            for u in range(2):
                for z2, z in ((z2_hi, z_hi), (z2_lo, z_lo)):
                    zt = z[:, u * P:(u + 1) * P].bitcast(f32)
                    nc.gpsimd.tensor_tensor(z2[:, u, :], zt, zt, ALU.add).then_inc(z2_made, 1)
            pool.wait_ge(sq_lo_made, SLABS)
            for u in range(2):
                nc.gpsimd.memset(top_v[u][:, :], 0.0).then_inc(tops_clear, 1)
                nc.gpsimd.memset(top_i[u][:, :], 0).then_inc(tops_clear, 1)
            pool.wait_ge(tops_clear, 4)

            def tile(at_tile, u, slab=None, q=None, single=None):
                wait_alone(pool, row_free, at_tile(1, 1))
                for kept, found in ((v_all, top_v), (i_all, top_i)):
                    nc.gpsimd.tensor_copy(kept[:, ds(at_tile(1), 1), :].rearrange("p a k -> p (a k)"),
                                          found[u][:, 0:TOPK]).then_inc(top_saved, 1)
                start = 0
                for i, (size, _, mine) in enumerate(CHUNKS[u]):
                    if mine:
                        wait_alone(pool, score_saved, at_tile(NCHUNKS, i + 1 + 2))
                        part = rows[u][:, start * SLAB:(start + size) * SLAB]
                        nc.gpsimd.tensor_scalar(part, part, 0.0, None, ALU.min).then_inc(clamped, 1)
                    start += size
                wait_alone(pool, score_ps, at_tile(NCHUNKS, NCHUNKS))
                for z2, z in ((z2_hi, z_hi), (z2_lo, z_lo)):
                    zt = z[:, ds(at_tile(P, 2 * P), P)].bitcast(f32)
                    nc.gpsimd.tensor_tensor(z2[:, u, :], zt, zt, ALU.add).then_inc(z2_made, 1)

            each_tile(pool, tile)
            for u in range(2):
                pool.wait_ge(row_free, TILES + 1 + u)
                nc.gpsimd.tensor_copy(v_all[:, TILES + u, :], top_v[u][:, 0:TOPK]).then_inc(top_saved, 1)
                nc.gpsimd.tensor_copy(i_all[:, TILES + u, :], top_i[u][:, 0:TOPK]).then_inc(top_saved, 1)
            pool.wait_ge(top_saved, 2 * (PADT + TILES))

            pool.wait_ge(w_stored, 16 * PARTS)

            def gathers(slab, first):
                if not first:
                    pool.wait_ge(gathered, slab * (16 * GATHERS))
                    wait_alone(pool, near_made, slab * QT)
                nc.gpsimd.tensor_copy(gather_i[:, :],
                                      i_all[:, ds(slab * QT + PADT, QT), :].rearrange("p a k -> p (a k)")
                                      ).then_inc(gather_i_made, 1)
                wait_alone(pool, gather_i_made, slab + 1)
                for c in range(GATHERS):
                    nc.gpsimd.indirect_dma_start(
                        gat[:, c * D:(c + 1) * D], None, w_table[:, :],
                        bass.IndirectOffsetOnAxis(ap=gather_i[:, c:c + 1], axis=0)).then_inc(gathered, 16)

            gathers(0, True)
            with pool.Fori(1, SLABS) as slab:
                gathers(slab, False)

        @block.scalar
        def _(act):
            act.sem_inc(d_row_made, TURN)
            act.sem_inc(part_saved, TURN)
            act.sem_inc(score_saved, 2)
            act.sem_inc(part_stored, 16 * TURN)
            act.wait_ge(const_made, CONSTANTS)
            act.wait_ge(b2_ps, 1)
            nc.scalar.activation(b2all[:, :], bank(4)[:, 0:D], ACT.Copy).then_inc(b2_made, 1)
            def root_of(slab):
                act.wait_ge(rowsum_ps, slab + (1 + TURN))
                nc.scalar.activation(root[:, 0:QT], row_ps[:, ds(slab * QT, QT)], ACT.Sqrt).then_inc(root_made, 1)

            def y_high(slab):
                wait_alone(act, y_made, slab + 1)
                nc.scalar.activation(y_hi[:, ds(slab * QT, QT), :], hw1[:, ds(slab * QT, QT), :],
                                     ACT.Copy).then_inc(y_hi_made, 1)

            def normalise(part):
                wait_alone(act, centred, part + 1)
                nc.scalar.activation(square[:, :, :], xn[:, ds(part * PREP_TILES, PREP_TILES), :],
                                     ACT.Square).then_inc(squared, 1)
                act.wait_ge(var_made, part + 1)
                nc.scalar.activation(std[:, :], var[:, :], ACT.Sqrt, bias=eps_ln[:, 0:1],
                                     scale=1.0 / D).then_inc(std_made, 1)

            def prepare(part):
                wait_alone(act, normed, part + 1)
                def relu(b):
                    nc.scalar.activation(hs[:, :, :], xn[:, ds(b * QT, QT), :], ACT.Relu).then_inc(h_made, 1)

                relu(part * BATCHES)
                for j in range(BATCHES):
                    b = part * BATCHES + j
                    act.wait_ge(hT_ps, b + 1)
                    nc.scalar.activation(hT[:, :], bank(4), ACT.Copy).then_inc(hT_made, 1)
                    if j < BATCHES - 1:
                        relu(b + 1)
                    wait_alone(act, hw_ps, b + 1)
                    both = bank(5, 2).rearrange("p (c w d) -> p c w d", c=QT, w=2)
                    nc.scalar.activation(hw1[:, ds(b * QT, QT), :], both[:, :, 0, :], ACT.Copy).then_inc(hw_saved, 1)
                    nc.scalar.activation(hw2_out[:, j * QT:(j + 1) * QT, :], both[:, :, 1, :],
                                         ACT.Copy).then_inc(hw_saved, 1)
                wait_alone(act, hw_saved, (part + 1) * (2 * BATCHES))
                act.dma_start(hw2_tiles[:, ds(part * PREP_TILES, PREP_TILES), :],
                              hw2_out[:, :, :]).then_inc(hw2_stored, 16)

            def sweep1(g, slab, first=False):
                prep = g * SPG < PREP_SLABS
                if not first:
                    root_of(slab - 1)
                if prep:
                    if not first:
                        wait_alone(act, hw2_stored, slab * 16)
                    normalise(slab)
                if first:
                    act.dma_start(xn[:, PREP_TILES:TILES, :], x_tiles[:, PREP_TILES:TILES, :]).then_inc(x_loaded, 16)
                else:
                    y_high(slab - 1)
                if prep:
                    prepare(slab)
                if g:
                    wait_alone(act, multiplied, (slab - SPG * g + 1) * known(g) + (MULT_CREDIT + mults_before(g)))
                    nc.scalar.activation(xu[:, ds(slab * SLAB, SLAB)],
                                         psum[:, ds((slab - SPG * g + SPG * (g % 2)) * SLAB, SLAB)],
                                         ACT.Copy).then_inc(partial_saved, 1)

            sweep1(0, 0, True)
            for g in range(GROUPS):
                with act.Fori(max(SPG * g, 1), SPG * (g + 1)) as slab:
                    sweep1(g, slab)

            def high_parts(this):
                arrived(act, this)
                for hf in range(HALVES):
                    act.wait_ge(halves, this[0] * HALVES + (hf + HALF_CREDIT - HIGHS + 1))
                    nc.scalar.activation(a_hi[:, (HALVES * this[2] + hf) % HIGHS, :],
                                         ring[:, this[2], hf * HALF:(hf + 1) * HALF],
                                         ACT.Copy).then_inc(hi_made, 1)

            def split_squares(slab):
                wait_alone(act, sq_ps, slab + 1)
                nc.scalar.activation(nsq[:, ds(slab * SLAB, SLAB)], bank(5), ACT.Copy)
                nc.scalar.activation(sq_col[:, ds(slab * QT, QT)], bank(6)[:, 0:QT], ACT.Copy, scale=-1.0)
                nc.scalar.activation(nsq_col[:, ds(slab * QT, QT)], bank(6)[:, 0:QT],
                                     ACT.Copy).then_inc(sq_hi_made, 1)
                wait_alone(act, sq_rest, slab + (1 + TURN))
                nc.scalar.activation(sq_mid[:, :], rest[:, :], ACT.Copy)
                nc.scalar.activation(nsq[32:64, ds(slab * SLAB, SLAB)], rest[32:64, :],
                                     ACT.Copy).then_inc(sq_mid_made, 1)

            def z_parts(slab):
                wait_alone(act, z_slab_made, slab + 1)
                nc.scalar.activation(z_hi[:, ds(slab * SLAB, SLAB)], z_slab[:, :], ACT.Copy).then_inc(z_hi_made, 1)
                nc.scalar.activation(zsq[:, :], z_slab[:, :], ACT.Square).then_inc(zsq_made, 1)

            for k in range(READS2 + 4):
                if k < READS2:
                    high_parts(split2(k))
                if k - 3 in start2[1:]:
                    split_squares(start2.index(k - 3) - 1)
                if k == 1:
                    root_of(SLABS - 1)
                if k == 4:
                    y_high(SLABS - 1)
                if k - 1 in start2:
                    slab = start2.index(k - 1)
                    if slab:
                        z_parts(slab - 1)
                    if slab < SLABS:
                        if slab:
                            act.wait_ge(z_scaled, slab)
                        act.wait_ge(d_row_ps, slab + (1 + TURN))
                        nc.scalar.activation(d_row[:, :], bank(4), ACT.Copy).then_inc(d_row_made, 1)

            def similarities(t):
                kv = kern[:, t, :].rearrange("p t k -> p (t k)")
                nc.scalar.activation(kv, v_all[:, PADT + t.start:PADT + t.stop, :].rearrange("p t k -> p (t k)"),
                                     ACT.Sqrt, bias=eps_dist[:, 0:1], scale=-1.0).then_inc(dist_made, 1)
                act.wait_ge(dist_made, 1 + (t.start > 0))
                nc.scalar.activation(kv, kv, ACT.Exp, scale=-0.5).then_inc(kern_made, 1)

            def roots(t):
                act.wait_ge(sum2_made, 1 + (t.start > 0))
                nc.scalar.activation(root[:, t], rowsum[:, t], ACT.Sqrt).then_inc(root2_made, 1)

            def save_part(slab, ps):
                wait_alone(act, halves, slab * (PART_QUADS * HALVES)
                           + ((READS2 + PART_QUADS) * HALVES + HALF_CREDIT))
                wait_alone(act, part_stored, slab * 16 + 16 * TURN)
                nc.scalar.activation(part_out[:, :], ps, ACT.Copy).then_inc(part_saved, 1)

            def tile(at_tile, u, slab=None, q=None, single=None):
                def negate(i):
                    act.wait_ge(score_saved, at_tile(NCHUNKS, i + 1 + 2))
                    start = sum(c[0] for c in CHUNKS[u][:i])
                    part = rows[u][:, start * SLAB:(start + CHUNKS[u][i][0]) * SLAB]
                    nc.scalar.activation(part, part, ACT.Copy, scale=-1.0).then_inc(negated, 1)

                if single == PART_TILES + 2:
                    act.wait_ge(top_saved, 2 * (PADT + PART_TILES))
                    similarities(slice(0, PART_TILES))
                if single == PART_TILES + 3:
                    roots(slice(0, PART_TILES))
                act.wait_ge(row_free, at_tile(1, 1))
                start = 0
                for i, (size, upper, pools) in enumerate(CHUNKS[u]):
                    if i == NCHUNKS - 1 and q == QT - 1:
                        save_part(slab, bank(7))
                    wait_alone(act, score_ps, at_tile(NCHUNKS, i + 1))
                    nc.scalar.activation(rows[u][:, start * SLAB:(start + size) * SLAB], bank(4 * upper, size),
                                         ACT.Identity if pools else ACT.Relu, scale=1.0 if pools else -1.0,
                                         bias=(nsq_col if pools else sq_col)[:, ds(at_tile(1), 1)]
                                         ).then_inc(score_saved, 1)
                    if i and not CHUNKS[u][i - 1][2] and CHUNKS[u][i - 1][0] == 4:
                        negate(i - 1)
                    if not pools and size < 4:
                        negate(i)
                    start += size

            each_tile(act, tile)
            act.wait_ge(top_saved, 2 * (PADT + TILES))
            similarities(slice(PART_TILES, TILES))
            roots(slice(PART_TILES, TILES))

            for part in range(1, PARTS):
                t = slice(part * PART_TILES, (part + 1) * PART_TILES)
                act.wait_ge(w_made, part + 1)
                nc.scalar.activation(w_hi[:, t, :], w_all[:, t, :], ACT.Copy).then_inc(w_hi_made, 1)
            def save_late(i):
                products_done(act, READS2 + (EARLY_SLABS + i + 1) * PART_QUADS)
                nc.scalar.activation(part_late[:, i * SLAB:(i + 1) * SLAB], bank(7 - i),
                                     ACT.Copy).then_inc(part_saved, 1)
            for i in range(SLABS - EARLY_SLABS - 1):
                save_late(i)
            products_done(act, READS2 + READS3)
            act.wait_ge(part_stored, 16 * (EARLY_SLABS + TURN))
            act.wait_ge(w_stored, 16)

            for pos in range(LAST_QUADS):
                high_parts(split3(0, pos))
                if pos == 0:
                    save_late(SLABS - EARLY_SLABS - 1)

            def out_to_sbuf(slab, odd):
                products_done(act, slab * LAST_QUADS + (READS2 + READS3 + LAST_QUADS))
                nc.scalar.activation(oT[:, :], bank(odd), ACT.Copy).then_inc(oT_made, 1)

            def last_pass(slab, odd):
                for pos in range(LAST_QUADS):
                    high_parts(split3(slab, pos))
                    if pos == 1:
                        out_to_sbuf(slab - 1, 1 - odd)
                    if pos == PART_QUADS + 1:
                        act.wait_ge(oT_ps, slab)

            last_pass(1, 1)
            with act.Fori(1, SLABS // 2) as pair:
                for odd in range(2):
                    last_pass(pair * 2 + odd, odd)
            out_to_sbuf(SLABS - 1, 1)

        @block.vector
        def _(dve):
            steps = [0]
            for signal in (folded, sq_rest):
                dve.sem_inc(signal, TURN)
            dve.sem_inc(added, ADD_CREDIT)

            def step(ins):
                steps[0] += 1
                ins.then_inc(dve_step, 1)
                dve.wait_ge(dve_step, steps[0])

            def inverse_root(dst, src, rt, nt):
                step(nc.vector.reciprocal(dst, rt))
                step(nc.vector.tensor_tensor(nt, dst, dst, ALU.mult))
                step(nc.vector.tensor_tensor(nt, nt, src, ALU.mult))
                step(nc.vector.tensor_scalar(nt, nt, -0.5, 1.5, ALU.mult, ALU.add))
                step(nc.vector.tensor_tensor(dst, dst, nt, ALU.mult))

            def degrees(slab):
                sums = row_ps[:, ds(slab * QT, QT)]
                inv, nt = inverse[:, 0:QT], newton[:, 0:QT]
                mine = [lambda: nc.vector.reciprocal(inv, root[:, 0:QT]),
                        lambda: nc.vector.tensor_tensor(nt, inv, inv, ALU.mult),
                        lambda: nc.vector.tensor_tensor(nt, nt, sums, ALU.mult),
                        lambda: nc.vector.tensor_scalar(nt, nt, -0.5, 1.5, ALU.mult, ALU.add),
                        lambda: nc.vector.tensor_tensor(deg[:, ds(slab * QT, QT)], inv, nt, ALU.mult)]
                wait_alone(dve, root_made, slab + 1)
                for i, ins in enumerate(mine):
                    ins().then_inc(newton_step, 1)
                    wait_alone(dve, newton_step, slab * len(mine) + (i + 1))
                dve.wait_ge(hw_saved, slab * 2 + 2)
                y = hw1[:, ds(slab * QT, QT), :]
                nc.vector.tensor_tensor(y, y, deg[:, ds(slab * QT, QT)].unsqueeze(2).to_broadcast([P, QT, D]),
                                        ALU.mult).then_inc(y_made, 1)

            LT = PREP_TILES
            for g in range(GROUPS):
                prep = g * SPG < PREP_SLABS
                def sweep1(slab, first=False):
                    if prep:
                        dve.wait_ge(x_loaded, 16 if first else 32)
                        xq = xn[:, ds(slab * LT, LT), :]
                        nc.vector.tensor_reduce(mean[:, :], xq, AX.X, ALU.add).then_inc(ln_step, 1)
                        dve.wait_ge(ln_step, slab * 3 + 1)
                        nc.vector.tensor_scalar(mean[:, :], mean[:, :], 1.0 / D, None, ALU.mult).then_inc(ln_step, 1)
                        dve.wait_ge(ln_step, slab * 3 + 2)
                        nc.vector.tensor_tensor(xq, xq, mean[:, :].unsqueeze(2).to_broadcast([P, LT, D]),
                                                ALU.subtract).then_inc(centred, 1)
                    arrived1(dve, slab, 0)
                    arrived1(dve, slab, 1)
                    dve.wait_ge(folded, slab * 2 + TURN)
                    nc.vector.tensor_tensor(acc[:, :], ring[:, 0, :], ring[:, 1, :], ALU.add).then_inc(added, 1)
                    for pos in range(2, QUADS):
                        arrived1(dve, slab, pos)
                        dve.wait_ge(added, slab * ADDS + (ADD_CREDIT + pos - 1))
                        nc.vector.tensor_tensor(acc[:, :], acc[:, :], ring[:, pos % RING, :],
                                                ALU.add).then_inc(added, 1)
                        if prep and pos == 3:
                            dve.wait_ge(squared, slab + 1)
                            nc.vector.tensor_reduce(var[:, :], square[:, :, :], AX.X, ALU.add).then_inc(var_made, 1)
                        if pos == 4 and not first:
                            degrees(slab - 1)
                        if prep and pos == 6:
                            dve.wait_ge(std_made, slab + 1)
                            nc.vector.reciprocal(var[:, :], std[:, :]).then_inc(ln_step, 1)
                            dve.wait_ge(ln_step, slab * 3 + 3)
                            nc.vector.tensor_tensor(xq, xq, var[:, :].unsqueeze(2).to_broadcast([P, LT, D]),
                                                    ALU.mult).then_inc(normed, 1)
                    dve.wait_ge(added, slab * ADDS + (ADD_CREDIT + ADDS))
                    nc.vector.tensor_tensor(half[:, :], acc[:, 0:BLOCK // 2], acc[:, BLOCK // 2:BLOCK],
                                            ALU.add).then_inc(folded, 1)
                    dve.wait_ge(folded, slab * 2 + (1 + TURN))
                    dve.wait_ge(rowsum_ps, slab + TURN)
                    nc.vector.tensor_tensor(colsum[:, :], half[:, 0:SLAB], half[:, SLAB:2 * SLAB],
                                            ALU.add).then_inc(folded, 1)

                if g == 0:
                    sweep1(0, True)
                with dve.Fori(max(SPG * g, 1), SPG * (g + 1)) as slab:
                    sweep1(slab)

            def low_parts(this):
                for hf in range(HALVES):
                    here = slice(hf * HALF, (hf + 1) * HALF)
                    dve.wait_ge(hi_made, this[3] * HALVES + (hf + 1))
                    nc.vector.tensor_tensor(ring_lo[:, this[2], here], ring[:, this[2], here],
                                            a_hi[:, (HALVES * this[2] + hf) % HIGHS, :].bitcast(f32),
                                            ALU.subtract).then_inc(lo_made, 1)

            def split_squares(slab):
                if slab:
                    dve.wait_ge(sq_lo_made, slab)
                dve.wait_ge(sq_hi_made, slab + 1)
                nc.vector.tensor_tensor(rest[:, :], bank(5), nsq[:, ds(slab * SLAB, SLAB)],
                                        ALU.subtract).then_inc(sq_rest, 1)
                dve.wait_ge(sq_mid_made, slab + 1)
                dve.wait_ge(sq_rest, slab + (1 + TURN))
                nc.vector.tensor_tensor(nsq[64:96, ds(slab * SLAB, SLAB)], rest[64:96, :], sq_mid[64:96, :],
                                        ALU.subtract).then_inc(sq_lo_made, 1)

            def z_of(slab):
                up = bank(slab % 4)
                dve.wait_ge(d_row_made, slab + (1 + TURN))
                products_done(dve, start2[slab + 1])
                if slab:
                    dve.wait_ge(zsq_made, slab)
                if slab >= SPG:
                    nc.vector.tensor_tensor(u_sum[:, :], up, xu[:, ds(slab * SLAB, SLAB)],
                                            ALU.add).then_inc(u_step, 1)
                    dve.wait_ge(u_step, slab - (SPG - 1))
                    nc.vector.tensor_tensor(u_sum[:, :], u_sum[:, :], d_row[:, :], ALU.mult).then_inc(z_scaled, 1)
                else:
                    nc.vector.tensor_tensor(u_sum[:, :], up, d_row[:, :], ALU.mult).then_inc(z_scaled, 1)
                dve.wait_ge(z_scaled, slab + 1)
                nc.vector.tensor_scalar(u_sum[:, :], u_sum[:, :], b1c[:, 0:1], None, ALU.add).then_inc(z_shifted, 1)
                dve.wait_ge(z_shifted, slab + 1)
                nc.vector.scalar_tensor_tensor(z_slab[:, :], u_sum[:, :], SLOPE, u_sum[:, :], ALU.mult,
                                               ALU.max).then_inc(z_slab_made, 1)

            def z_low(slab):
                dve.wait_ge(z_hi_made, slab + 1)
                nc.vector.tensor_tensor(z_lo[:, ds(slab * SLAB, SLAB)], z_slab[:, :],
                                        z_hi[:, ds(slab * SLAB, SLAB)].bitcast(f32),
                                        ALU.subtract).then_inc(z_made, 1)

            dve.wait_ge(partial_saved, SLABS - SPG)
            dve.wait_ge(hw2_stored, 16 * PREPS)
            for k in range(READS2 + 4):
                if k < QUADS:
                    dve.wait_ge(y_hi_made, k + 1)
                    t = slice(k * QT, (k + 1) * QT)
                    nc.vector.tensor_tensor(y_lo[:, t, :], hw1[:, t, :], y_hi[:, t, :].bitcast(f32),
                                            ALU.subtract).then_inc(y_lo_made, 1)
                if k < READS2:
                    low_parts(split2(k))
                if k == 2:
                    degrees(SLABS - 1)
                    nc.vector.tensor_copy(rowsum[:, :], row_ps).then_inc(rowsum_saved, 1)
                if k - 3 in start2[1:]:
                    split_squares(start2.index(k - 3) - 1)
                if k in start2[1:]:
                    z_of(start2.index(k) - 1)
                if k - 1 in start2[1:]:
                    z_low(start2.index(k - 1) - 1)

            dve.wait_ge(sq_lo_made, SLABS)
            dve.wait_ge(tops_clear, 4)
            dve.sem_inc(row_free, 2)

            def degrees2(t):
                dve.wait_ge(root2_made, 1 + (t.start > 0))
                inverse_root(deg2[:, t], rowsum[:, t], root[:, t], newton[:, t])

            def sums2(t):
                dve.wait_ge(kern_made, 1 + (t.start > 0))
                step(nc.vector.tensor_reduce(near_sum[:, t], kern[:, t, :], AX.X, ALU.add))
                nc.vector.tensor_tensor(rowsum[:, t], rowsum[:, t], near_sum[:, t], ALU.add).then_inc(sum2_made, 1)
                dve.wait_ge(sum2_made, 1 + (t.start > 0))

            def tile(at_tile, u, slab=None, q=None, single=None):
                if single == PART_TILES + 2:
                    dve.wait_ge(rowsum_saved, 1)
                    sums2(slice(0, PART_TILES))
                if single == PART_TILES + 3:
                    degrees2(slice(0, PART_TILES))
                    dve.wait_ge(hw2_loaded, 16)
                    scale_w(0)
                dve.wait_ge(negated, at_tile(NCHUNKS - CLAMPS, NCHUNKS - CLAMPS))
                wait_alone(dve, clamped, at_tile(CLAMPS, CLAMPS))
                nc.vector.max(top_v[u][:, :], rows[u][:, :]).then_inc(max_found, 1)
                wait_alone(dve, max_found, at_tile(1, 1))
                nc.vector.max_index(top_i[u][:, :], top_v[u][:, :], rows[u][:, :]).then_inc(row_free, 1)

            def scale_w(part):
                t = slice(part * PART_TILES, (part + 1) * PART_TILES)
                w = w_all[:, t, :] if part else w_first[:, :, :]
                nc.vector.tensor_tensor(w, w, deg2[:, t].unsqueeze(2).to_broadcast([P, PART_TILES, D]),
                                        ALU.mult).then_inc(w_made, 1)

            def low_w(part):
                t = slice(part * PART_TILES, (part + 1) * PART_TILES)
                dve.wait_ge(w_hi_made, part)
                nc.vector.tensor_tensor(w_lo[:, t, :], w_all[:, t, :], w_hi[:, t, :].bitcast(f32),
                                        ALU.subtract).then_inc(w_lo_made, 1)

            each_tile(dve, tile)
            sums2(slice(PART_TILES, TILES))
            degrees2(slice(PART_TILES, TILES))
            dve.wait_ge(hw2_loaded, 16 * PARTS)
            for part in range(1, PARTS):
                scale_w(part)
                if part > 1:
                    low_w(part - 1)
            low_w(PARTS - 1)

            def neighbour(slab, c):
                if c == 0:
                    dve.wait_ge(gathered, slab * (16 * GATHERS) + 16 * GATHERS)
                rows_c = gat[:, c * TOPK * D:(c + 1) * TOPK * D]
                g3 = rows_c.rearrange("p (k d) -> p k d", d=D)
                weights = kern[:, ds(slab * QT + c, 1), :].rearrange("p t k -> p (t k)")
                nc.vector.tensor_tensor(g3, g3, weights.unsqueeze(2).to_broadcast([P, TOPK, D]),
                                        ALU.mult).then_inc(near_step, 1)
                wait_alone(dve, near_step, slab * QT + (c + 1))
                nc.vector.tensor_reduce(near[:, c * D:(c + 1) * D], rows_c.rearrange("p (k d) -> p d k", d=D),
                                        AX.X, ALU.add).then_inc(near_made, 1)

            def output(slab, stage):
                m3 = mix[:, :].rearrange("p (c d) -> p c d", d=D)
                if stage == 0:
                    dve.wait_ge(near_made, slab * QT + QT)
                    dve.wait_ge(oT_ps, slab + 1)
                    nc.vector.tensor_tensor(mix[:, :], bank(4), near[:, :], ALU.add).then_inc(mix_step, 1)
                elif stage == 1:
                    wait_alone(dve, mix_step, slab * 3 + 1)
                    nc.vector.tensor_tensor(m3, m3, deg2[:, ds(slab * QT, QT)].unsqueeze(2).to_broadcast([P, QT, D]),
                                            ALU.mult).then_inc(mix_step, 1)
                elif stage == 2:
                    dve.wait_ge(mix_step, slab * 3 + 2)
                    nc.vector.tensor_tensor(m3, m3, b2all[:, :].unsqueeze(1).to_broadcast([P, QT, D]),
                                            ALU.add).then_inc(mix_step, 1)
                else:
                    dve.wait_ge(mix_step, slab * 3 + 3)
                    dve.wait_ge(xs_loaded, slab * 16 + 16)
                    nc.vector.tensor_tensor(outs[:, :], mix[:, :], xs[:, :], ALU.add).then_inc(outs_made, 1)

            for pos in range(LAST_QUADS):
                low_parts(split3(0, pos))

            def last_pass(slab):
                for pos in range(LAST_QUADS):
                    low_parts(split3(slab, pos))
                    if 2 <= pos < 2 + QT:
                        neighbour(slab - 1, pos - 2)
                    if QUADS // 2 <= pos < QUADS // 2 + 4:
                        output(slab - 1, pos - QUADS // 2)

            last_pass(1)
            with dve.Fori(1, SLABS // 2) as pair:
                for odd in range(2):
                    last_pass(pair * 2 + odd)
            for c in range(QT):
                neighbour(SLABS - 1, c)
            for stage in range(4):
                output(SLABS - 1, stage)

        @block.tensor
        def _(pe):
            for signal in (rowsum_ps, d_row_ps):
                pe.sem_inc(signal, TURN)
            pe.wait_ge(const_made, CONSTANTS)
            pe.wait_ge(small_loaded, 64)
            nc.tensor.matmul(bank(4)[:, 0:D], ones[:, :], b2row[:, :], start=True, stop=True).then_inc(b2_ps, 1)
            pe.wait_ge(b2_made, 1)
            pe.sem_inc(multiplied, MULT_CREDIT)
            pe.sem_inc(halves, HALF_CREDIT)

            def prepare(b):
                pe.wait_ge(h_made, b + 1)
                for c in range(QT):
                    ins = nc.tensor.transpose(bank(4)[:, c * P:(c + 1) * P], hs[:, c, :], ident[:, :])
                ins.then_inc(hT_ps, 1)
                pe.wait_ge(hT_made, b + 1)
                for c in range(QT):
                    ins = nc.tensor.matmul(bank(5, 2)[:, c * 2 * D:(c + 1) * 2 * D], hT[:, c * P:(c + 1) * P],
                                           w12[:, :, :].rearrange("p w d -> p (w d)"), start=True, stop=True)
                ins.then_inc(hw_ps, 1)

            def product(dst, q, slot, first, last):
                for c in range(QT):
                    ins = nc.tensor.matmul(dst, hw1[:, q * QT + c, :], ring[:, slot, c * SLAB:(c + 1) * SLAB],
                                           start=first and c == 0, stop=last and c == QT - 1)
                ins.then_inc(multiplied, 1)

            for g in range(GROUPS):
                if g > 2:
                    pe.wait_ge(partial_saved, SPG * (g - 2))
                with pe.Fori(SPG * g, SPG * (g + 1)) as slab:
                    if g * SPG < PREP_SLABS:
                        for j in range(BATCHES):
                            prepare(slab * BATCHES + j)
                    dst = psum[:, ds((slab - SPG * g + SPG * (g % 2)) * SLAB, SLAB)]
                    for pos, (q, mult) in enumerate(order1(g)):
                        if mult:
                            pe.wait_ge(y_made, q + 1)
                            arrived1(pe, slab, pos)
                            product(dst, q, pos % RING, q == 0, q == known(g) - 1)
                    pe.wait_ge(folded, slab * 2 + (2 + TURN))
                    for c in range(QT):
                        ins = nc.tensor.matmul(row_ps[:, ds(slab * QT + c, 1)], colsum[:, c * P:(c + 1) * P],
                                               ones[:, 0:1], start=True, stop=True)
                    ins.then_inc(rowsum_ps, 1)

            def split_product(dst, v_hi, v_lo, q, this, first, last):
                for hf in range(HALVES):
                    turn = this[3] * HALVES + (hf + 1)
                    pe.wait_ge(hi_made, turn)
                    for c in range(QT // HALVES):
                        t = q * QT + hf * (QT // HALVES) + c
                        cols = a_hi[:, (HALVES * this[2] + hf) % HIGHS, c * SLAB:(c + 1) * SLAB]
                        nc.tensor.matmul(dst, v_hi[:, t, :], cols, start=first and hf == 0 and c == 0, stop=False)
                        nc.tensor.matmul(dst, v_lo[:, t, :], cols, start=False, stop=False)
                    pe.wait_ge(lo_made, turn)
                    for c in range(QT // HALVES):
                        t = q * QT + hf * (QT // HALVES) + c
                        i = hf * HALF + c * SLAB
                        ins = nc.tensor.matmul(dst, v_hi[:, t, :], ring_lo[:, this[2], i:i + SLAB], start=False,
                                               stop=last and hf == HALVES - 1 and c == QT // HALVES - 1)
                    ins.then_inc(halves, 1)

            def squares(slab):
                pe.wait_ge(zsq_made, slab + 1)
                pe.wait_ge(sq_rest, slab + TURN)
                nc.tensor.matmul(bank(5), neg_ones[:, :], zsq[:, :], start=True, stop=True)
                for c in range(QT):
                    ins = nc.tensor.matmul(bank(6)[:, c:c + 1], zsq[:, c * P:(c + 1) * P], neg_ones[:, 0:1],
                                           start=True, stop=True)
                ins.then_inc(sq_ps, 1)

            pe.wait_ge(partial_saved, SLABS - SPG)
            for k in range(READS2 + 2):
                if k < READS2:
                    slab, q = blocks2[k]
                    first, last = k == start2[slab], k + 1 == start2[slab + 1]
                    if k < QUADS:
                        pe.wait_ge(y_lo_made, k + 1)
                    if first and slab >= 4:
                        pe.wait_ge(z_scaled, slab - 3)
                    split_product(bank(slab % 4), y_hi, y_lo, q, split2(k), first, last)
                    if first:
                        pe.wait_ge(diag_made, slab + 1)
                        pe.wait_ge(d_row_made, slab + TURN)
                        nc.tensor.matmul(bank(4), ones[:, :], diag[:, :], start=True, stop=True).then_inc(d_row_ps, 1)
                if k - 1 in start2[1:]:
                    squares(start2.index(k - 1) - 1)

            def early_product(dst, slab, q):
                this = early(slab, q)
                arrived(pe, this)
                for c in range(QT):
                    ins = nc.tensor.matmul(dst, w_first[:, q * QT + c, :], ring[:, this[2], c * SLAB:(c + 1) * SLAB],
                                           start=q == 0 and c == 0, stop=q == PART_QUADS - 1 and c == QT - 1)
                ins.then_inc(halves, HALVES)

            def tile(at_tile, u, slab=None, q=None, single=None):
                pe.wait_ge(z2_made, at_tile(2, 2))
                start = 0
                for i, (size, upper, _) in enumerate(CHUNKS[u]):
                    if u == 0 and i == 1:
                        pe.wait_ge(sq_lo_made, SLABS)
                        pe.wait_ge(z_made, SLABS)
                    if i == NCHUNKS - 1 and slab is not None:
                        if q == 0:
                            pe.wait_ge(part_saved, slab + TURN)
                            pe.wait_ge(w_made, 1)
                        early_product(bank(7), slab, q)
                    pe.wait_ge(score_saved, at_tile(NCHUNKS, i + 1))
                    cols = [slice((start + c) * SLAB, (start + c + 1) * SLAB) for c in range(size)]
                    for c, j in enumerate(cols):
                        nc.tensor.matmul(bank(4 * upper + c), z2_hi[:, u, :], z_hi[:, j], start=True, stop=False)
                        nc.tensor.matmul(bank(4 * upper + c), z2_hi[:, u, :], z_lo[:, j], start=False, stop=False)
                    for c, j in enumerate(cols):
                        nc.tensor.matmul(bank(4 * upper + c), z2_lo[:, u, :], z_hi[:, j], start=False, stop=False)
                    for c, j in enumerate(cols):
                        ins = nc.tensor.matmul(bank(4 * upper + c), part_rows[:, :],
                                               nsq[:, j], start=False, stop=True)
                    ins.then_inc(score_ps, 1)
                    start += size

            pe.wait_ge(z_scaled, SLABS)
            pe.wait_ge(z_made, CHUNKS[0][0][0])
            each_tile(pe, tile)
            pe.wait_ge(part_saved, EARLY_SLABS + TURN)
            for q in range(PART_QUADS):
                early_product(bank(7), EARLY_SLABS, q)
            pe.wait_ge(score_saved, 2 + TILES * NCHUNKS)
            with pe.Fori(EARLY_SLABS + 1, SLABS) as slab:
                for q in range(PART_QUADS):
                    early_product(psum[:, ds(slab * -SLAB + (EARLY_SLABS + 7) * SLAB, SLAB)], slab, q)

            def transposes(slab, first=False):
                pe.wait_ge(oT_made, slab + 1)
                if not first:
                    pe.wait_ge(outs_made, slab)
                pe.wait_ge(part_loaded, slab * 16 + 16)
                for c in range(QT):
                    here = slice(c * P, (c + 1) * P)
                    nc.tensor.matmul(bank(4)[:, here], oT[:, here], ident[:, :], start=True, stop=False)
                    ins = nc.tensor.matmul(bank(4)[:, here], part_in[:, here], ident[:, :], start=False, stop=True)
                ins.then_inc(oT_ps, 1)

            def last_pass(slab, odd, first=False):
                for pos in range(LAST_QUADS):
                    split_product(bank(odd), w_hi, w_lo, PART_QUADS + pos, split3(slab, pos), pos == 0,
                                  pos == LAST_QUADS - 1)
                    if pos == PART_QUADS - 1:
                        transposes(slab - 1, first)

            pe.wait_ge(w_lo_made, PARTS - 1)
            for pos in range(LAST_QUADS):
                split_product(bank(0), w_hi, w_lo, PART_QUADS + pos, split3(0, pos), pos == 0, pos == LAST_QUADS - 1)
            last_pass(1, 1, True)
            with pe.Fori(1, SLABS // 2) as pair:
                for odd in range(2):
                    last_pass(pair * 2 + odd, odd)
            transposes(SLABS - 1)


def kernel(x, adj, L0_gnn_W1, L0_gnn_b1, L0_gnn_W2, L0_gnn_b2):
    import concourse.bacc as bacc
    from concourse.bass_utils import run_bass_kernel_spmd

    at = np.asarray(adj).T.reshape(QUADS, QT, P, SLABS, SLAB)
    at = np.ascontiguousarray(at.transpose(3, 0, 2, 1, 4)).reshape(SLABS, QUADS, P, BLOCK)
    arrays = {
        "x": np.ascontiguousarray(x), "at_blocks": at,
        "w1": np.ascontiguousarray(L0_gnn_W1), "b1": np.ascontiguousarray(L0_gnn_b1),
        "w2": np.ascontiguousarray(L0_gnn_W2), "b2": np.ascontiguousarray(L0_gnn_b2),
    }
    nc = bacc.Bacc("TRN2", target_bir_lowering=False, num_devices=1, dynamic_dma_scratch_size=8192)
    f32 = mybir.dt.float32
    aps = {k: nc.dram_tensor(k, list(a.shape), f32, kind="ExternalInput").ap() for k, a in arrays.items()}
    out = nc.dram_tensor("out", [N, D], f32, kind="ExternalOutput").ap()
    w_table = nc.dram_tensor("w_table", [N, D], f32, kind="Internal").ap()
    partials = nc.dram_tensor("partials", [P, N], f32, kind="Internal").ap()
    hw2_table = nc.dram_tensor("hw2_table", [N, D], f32, kind="Internal").ap()
    build(nc, **aps, out=out, w_table=w_table, hw2_table=hw2_table, partials=partials)
    r = run_bass_kernel_spmd(nc, [arrays], core_ids=[0])
    return r.results[0]["out"]
```
